# Optimizing a Trainium2 kernel written in Bass

```python
import numpy as np
import jax
import jax.numpy as jnp

def _softmax(x, axis=-1):
    return jax.nn.softmax(x, axis=axis)

def _gelu(x):
    return jax.nn.gelu(x, approximate=True)

def _silu(x):
    return jax.nn.silu(x)

def _sigmoid(x):
    return jax.nn.sigmoid(x)

def _layernorm(x, axis=-1, eps=1e-05):
    m = jnp.mean(x, axis=axis, keepdims=True)
    v = jnp.var(x, axis=axis, keepdims=True)
    return (x - m) / jnp.sqrt(v + eps)

def _scatter_add(tgt, idx, src, axis=0):
    return tgt.at[idx].add(src)

def _segment_sum(src, seg, n):
    return jax.ops.segment_sum(src, seg, n)
kernel_name = 'mk_adj_resnorm_d1_adj_r2_0559c7'

def setup_inputs(seed: int=0):
    np.random.seed(seed)
    _w = jnp.asarray

    def _rec_inputs():
        import jax
        import jax.numpy as jnp
        _gk = jax.random.key(seed)
        x = -0.0002928 + 1 * jax.random.normal(jax.random.fold_in(_gk, 1), (8192, 256), jnp.float32)
        _w = (1.0 + jnp.arange(8192, dtype=jnp.float32)) ** (-0.5)
        _w = _w / _w.mean()
        _pij = jnp.clip(0.000488281 * _w[:, None] * _w[None, :], 0.0, 1.0)
        _a = jax.random.uniform(jax.random.fold_in(_gk, 2), (8192, 8192)) < _pij
        adj = _a.astype(jnp.int32)
        return (x, adj)
    x, adj = _rec_inputs()

    def _L0_gnn_setup():
        import jax, jax.numpy as jnp
        import numpy as np
        EPS = 1e-08
        key = jax.random.key(seed)
        k1, k2, k3 = jax.random.split(key, 3)
        N, IN_DIM, OUT_DIM = (4096, 256, 256)
        h = jax.random.normal(k1, (N, IN_DIM), dtype=jnp.float32)
        adj = jax.random.randint(k2, (N, N), 0, 2, dtype=jnp.int32)
        W = jax.random.normal(k3, (OUT_DIM, IN_DIM), dtype=jnp.float32) * (1.0 / np.sqrt(IN_DIM))
        return {'h': h, 'adj': adj, 'W': W}
    _L0_gnn_all = _L0_gnn_setup()
    _L0_gnn_in = {k: v for k, v in _L0_gnn_all.items() if k in ('W',)}
    del _L0_gnn_all
    return {'x': x, 'adj': adj, 'L0_gnn_W': _L0_gnn_in['W']}

def reference(x, adj, L0_gnn_W):
    import jax
    import jax.numpy as jnp

    def _L0_gnn_ref(h, adj, W):
        import jax, jax.numpy as jnp
        import numpy as np
        EPS = 1e-08
        Wh = h @ W.T
        N = Wh.shape[0]
        norms = jnp.linalg.norm(Wh, axis=1, keepdims=True)
        sim = Wh @ Wh.T / (norms * norms.T + EPS)
        mask = (adj > 0) | jnp.eye(N, dtype=bool)
        sim_masked = jnp.where(mask, sim, -jnp.inf)
        alpha = jax.nn.softmax(sim_masked, axis=1)
        return alpha @ Wh
    x = _layernorm(x + _L0_gnn_ref(x, adj, L0_gnn_W), axis=-1)
    return x

_drawn_inputs = setup_inputs


def setup_inputs(seed=0):
    import zlib

    import numpy as np

    out = dict(_drawn_inputs(seed))
    spreads = {}
    factors = {}
    for name, (base, spread) in spreads.items():
        noise = np.random.default_rng([zlib.crc32(name.encode()), seed]).standard_normal(out[name].shape)
        drawn = base * np.exp(spread * noise) if base else spread * noise
        out[name] = jnp.asarray(drawn.astype(out[name].dtype))
    for name, factor in factors.items():
        out[name] = (out[name] * factor).astype(out[name].dtype)
    return out
```

```python
from contextlib import ExitStack

import numpy as np
import concourse.bass as bass
from concourse import mybir

F32 = mybir.dt.float32
F32R = mybir.dt.float32r
BF16 = mybir.dt.bfloat16
I32 = mybir.dt.int32
U32 = mybir.dt.uint32
ALU = mybir.AluOpType
ACT = mybir.ActivationFunctionType
AX = mybir.AxisListType

P = 128
N = 8192
D = 256
KD = D // P
NT = N // P
NQ = 4
QC = N // NQ
QB = QC // P
BITS = 16
G = P // BITS
RND = 8
PAIRS = RND // 2
TW = D + 2
ONE, RN = D, D + 1
P0 = 8
RING = 4
EPS_LN = 1e-5
TINY = 1e-36
MASKED = -3e38

C_ID, C_BLK, C_PACK, C_LANE = 0, P, P + NT, P + NT + G
C_HALF, C_TINY, C_EPS, C_F = C_LANE + 1, C_LANE + 2, C_LANE + 3, C_LANE + 4
I_BIT, I_DIAG, I_N = 0, BITS, BITS + G


def build(nc, xT, x, adj, wT, cf, ci, out):
    table = nc.dram_tensor("table", (N, TW), F32).ap()
    ctx = ExitStack()
    with ctx:
        def sb(name, shape, dt):
            return ctx.enter_context(nc.sbuf_tensor(name, shape, dt))

        def sem(name):
            return ctx.enter_context(nc.semaphore(name))

        whT = sb("whT", [P, KD, N], F32)
        adj_sb = sb("adj_sb", [P, 2, NQ, QC], I32)
        mask = sb("mask", [P, NQ, QC], BF16)
        bias = sb("bias", [P, 2, N], BF16)
        gat = sb("gat", [P, RND, TW], F32)
        gT = sb("gT", [P, 2, KD, 2, P], F32)
        prob = sb("prob", [P, 2, 2, P], F32)
        words = sb("words", [P, G, NT], I32)
        keys = sb("keys", [P, G, NT], F32)
        base = sb("base", [P, NT], F32)
        used = sb("used", [P, NT], F32)
        count = sb("count", [P, 1], F32)
        most = sb("most", [1, 2], I32)
        topb = sb("topb", [P, RND], F32)
        topk = sb("topk", [P, G, RND], F32)
        topi = sb("topi", [P, G, RND], I32)
        bits = sb("bits", [P, RND, G, BITS], I32)
        rows = sb("rows", [P, 2, NT], U32)
        rows_now = sb("rows_now", [P, RND], U32)
        x_sb = sb("x_sb", [P, 2, D], F32)
        yz = sb("yz", [P, 4, D], F32)
        den = sb("den", [P, 2], F32)
        stats = sb("stats", [P, 6], F32)
        mv = sb("mv", [P, 2, 2], F32)
        rstd = sb("rstd", [P, 2, 2], F32)
        cf_sb = sb("cf_sb", [P, C_F], F32)
        ci_sb = sb("ci_sb", [P, I_N], I32)
        idb = sb("idb", [P, P], BF16)
        idr = sb("idr", [P, P], F32R)
        packw = sb("packw", [P, G], BF16)
        zeros = sb("zeros", [P, P], BF16)
        ssq = sb("ssq", [P, P0], F32)
        ssg = sb("ssg", [P, P0], F32)

        wT_sb = mask[:, 0, 0:2 * KD * D].bitcast(F32).rearrange("p (k o) -> p k o", k=KD)
        ident = cf_sb[:, C_ID:C_ID + P]
        y_sb, z_sb = yz[:, 0:2, :], yz[:, 2:4, :]
        x_ring = yz[:, :, :].rearrange("p r (k n) -> p r k n", k=KD)
        unit = prob[:, :, :, :].rearrange("p a b c -> p a (b c)")
        tab = adj_sb[:, 1, NQ - 1, :].bitcast(F32)[:, 0:RING * TW].rearrange("p (r w) -> p r w", r=RING)
        junk = gT[:, 0, 0, :, :].rearrange("p b c -> p (b c)")

        def bank(name):
            return ctx.enter_context(nc.psum_tensor(name, [P, 512], F32))

        words_ps = [bank("words0"), bank("words1")]
        gT_ps = [bank("gT0"), bank("gT1")]
        s_ps = [bank("s0"), bank("s1")]
        o_ps = [bank("o0"), bank("o1")]

        consts_in = sem("consts_in")
        consts_ready = sem("consts_ready")
        x_in = [sem(f"x_in{k}") for k in range(RING)]
        wh_done = sem("wh_done")
        tab_copied = sem("tab_copied")
        ss_ready = sem("ss_ready")
        r_ready = sem("r_ready")
        unit_ready = sem("unit_ready")
        unitT_done = sem("unitT_done")
        unitT_saved = sem("unitT_saved")
        tab_stored = [sem(f"tab_stored{k}") for k in range(RING)]
        table_ready = sem("table_ready")
        adj_in = [[sem(f"adj_in{a}{q}") for q in range(NQ)] for a in range(2)]
        conv_done = sem("conv_done")
        packed = sem("packed")
        count_ready = sem("count_ready")
        countT_done = sem("countT_done")
        sel_done = sem("sel_done")
        g_ready = [sem(f"g_ready{b}") for b in range(PAIRS)]
        g_free = [sem(f"g_free{b}") for b in range(PAIRS)]
        gT_done = sem("gT_done")
        gT_saved = sem("gT_saved")
        s_done = sem("s_done")
        prob_ready = sem("prob_ready")
        tile_done = sem("tile_done")
        res_in = [sem("res_in0"), sem("res_in1")]
        y_read = sem("y_read")
        var_ready = sem("var_ready")
        rstd_ready = sem("rstd_ready")
        z_ready = sem("z_ready")
        stored = [sem("stored0"), sem("stored1")]
        dve_step = sem("dve_step")
        pool_step = sem("pool_step")

        def pairs_of(eng, a, tile_no):
            selected = eng.snap(tile_no)
            eng.wait_ge(consts_in, 48)
            eng.wait_ge(sel_done, selected)
            top = eng.value_load(most[0:1, a:a + 1], min_val=1, max_val=NT)
            eng.reg_add(tile_no, tile_no, 1)
            return eng.snap((top + 1) >> 1)

        def wait(eng, s, value):
            if not isinstance(value, int) or value > 0:
                eng.wait_ge(s, value)

        def tiles(eng, body):
            for t in range(3):
                body(t, t % 2)
            with eng.Fori(0, (NT - 4) // 2) as i:
                body(2 * i + 3, 1)
                body(2 * i + 4, 0)
            body(NT - 1, (NT - 1) % 2)

        def round_of(r):
            return nc.s_assert_within(r, 0, NT // RND - 1, skip_runtime_bounds_check_because="a lane has 64 columns")

        def half(t):
            return t // 2 if isinstance(t, int) else (t >> 1)

        block = ctx.enter_context(nc.Block())

        @block.sync
        def _(sp):
            sp.dma_start(cf_sb[:, :], cf).then_inc(consts_in, 16)
            sp.dma_start(ci_sb[:, :], ci).then_inc(consts_in, 16)
            sp.dma_start(wT_sb[:, :, :], wT.rearrange("(k p) o -> p k o", p=P)).then_inc(consts_in, 16)

            def load_adj(t, a, q):
                wait(sp, conv_done, NQ * t + q + 1 - 2 * NQ)
                sp.dma_start(adj_sb[:, a, q, :], adj[bass.ds(t * P, P), q * QC:(q + 1) * QC]).then_inc(adj_in[a][q], 16)

            def project(i):
                for k in range(P0):
                    m = P0 * i + k
                    wait(sp, wh_done, m - 3)
                    sp.dma_start(x_ring[:, k % RING, :, :], xT[bass.ds(m, 1), :, :, :].rearrange("a p k n -> (a p) k n")).then_inc(x_in[k % RING], 16)
                    if k >= 2:
                        store(i, k - 2)
                store(i, P0 - 2)
                store(i, P0 - 1)

            def store(i, k):
                m = P0 * i + k
                sp.wait_ge(r_ready, m + 1)
                sp.dma_start(table[bass.ds(m * P, P), :], tab[:, k % RING, :]).then_inc(tab_stored[k % RING], 16)

            project(0)
            load_adj(0, 0, 0)
            load_adj(0, 0, 1)
            with sp.Fori(1, 4) as i:
                project(i)
            load_adj(0, 0, 2)
            load_adj(0, 0, 3)
            load_adj(1, 1, 0)
            with sp.Fori(4, P0) as i:
                project(i)
            load_adj(1, 1, 1)
            load_adj(1, 1, 2)
            for k in range(RING):
                sp.wait_ge(tab_stored[k], 16 * NT // RING)
            sp.sem_inc(table_ready, 1)
            sp.wait_ge(unit_ready, NT)
            load_adj(1, 1, 3)

            def load_res(t, a):
                wait(sp, y_read, t - 1)
                sp.dma_start(x_sb[:, a, :], x[bass.ds(t * P, P), :]).then_inc(res_in[a], 16)

            def store_out(t, a):
                sp.wait_ge(z_ready, t + 1)
                sp.dma_start(out[bass.ds(t * P, P), :], z_sb[:, a, :]).then_inc(stored[a], 16)

            for t in range(2, 6):
                for q in range(NQ):
                    load_adj(t, t % 2, q)
                load_res(t - 2, t % 2)
            with sp.Fori(3, NT // 2) as i:
                for a in range(2):
                    for q in range(NQ):
                        load_adj(2 * i + a, a, q)
                    load_res(2 * i + a - 2, a)
                    store_out(2 * i + a - 6, a)
            for t in range(NT - 6, NT):
                if t >= NT - 2:
                    load_res(t, t % 2)
            for t in range(NT - 6, NT):
                store_out(t, t % 2)
            for a in range(2):
                sp.wait_ge(stored[a], 16 * NT // 2)

        @block.gpsimd
        def _(pool):
            pool.memset(gat[:, :, :], 0.0).then_inc(consts_ready, 1)
            pool.memset(tab[:, :, ONE:ONE + 1], 1.0).then_inc(pool_step, 1)
            pool.memset(zeros[:, :], 0.0).then_inc(consts_ready, 1)

            def project(i):
                for k in range(P0):
                    m = P0 * i + k
                    pool.sem_clear(pool_step)
                    pool.wait_ge(ss_ready, m + 1)
                    pool.tensor_tensor(ssg[:, k:k + 1], ssq[:, k:k + 1], cf_sb[:, C_TINY:C_TINY + 1], ALU.add).then_inc(pool_step, 1)
                    pool.wait_ge(pool_step, 1)
                    pool.tensor_tensor(tab[:, k % RING, RN:RN + 1], ssg[:, k:k + 1], cf_sb[:, C_HALF:C_HALF + 1], ALU.pow).then_inc(r_ready, 1)

            pool.wait_ge(pool_step, 1)
            pool.wait_ge(consts_in, 48)
            project(0)
            with pool.Fori(1, P0) as i:
                project(i)

            pool.wait_ge(table_ready, 1)
            tile_no = pool.alloc_register("tile_no")
            pool.reg_mov(tile_no, 1)
            uses = [pool.alloc_register(f"uses{b}") for b in range(PAIRS)]
            for u in uses:
                pool.reg_mov(u, 1)

            def gather(a, r, b):
                pool.sem_clear(pool_step)
                pool.wait_ge(g_free[b], pool.snap(uses[b]))
                pool.tensor_copy(rows_now[:, 2 * b:2 * b + 2], rows[:, a, bass.ds(r * RND + 2 * b, 2)]).then_inc(pool_step, 1)
                pool.wait_ge(pool_step, 1)
                for s in range(2 * b, 2 * b + 2):
                    pool.indirect_dma_start(
                        out=gat[:, s, :], out_offset=None, in_=table,
                        in_offset=bass.IndirectOffsetOnAxis(ap=rows_now[:, s:s + 1], axis=0),
                        bounds_check=N - 1, oob_is_err=False).then_inc(g_ready[b], 16)
                pool.reg_add(uses[b], uses[b], 1)

            def inverse_dev(t, a):
                pool.sem_clear(pool_step)
                pool.wait_ge(var_ready, t + 1)
                pool.tensor_tensor(rstd[:, a, 0:1], mv[:, a, 1:2], cf_sb[:, C_EPS:C_EPS + 1], ALU.add).then_inc(pool_step, 1)
                pool.wait_ge(pool_step, 1)
                pool.tensor_tensor(rstd[:, a, 1:2], rstd[:, a, 0:1], cf_sb[:, C_HALF:C_HALF + 1], ALU.pow).then_inc(rstd_ready, 1)

            def tile(t, a):
                if not isinstance(t, int) or t >= 3:
                    inverse_dev(t - 3, 1 - a)
                pairs = pairs_of(pool, a, tile_no)
                with pool.Fori(0, (pairs + (PAIRS - 1)) >> 2) as r:
                    r = round_of(r)
                    gather(a, r, 0)
                    for b in range(1, PAIRS):
                        with pool.If(r * PAIRS + b < pairs):
                            gather(a, r, b)

            tiles(pool, tile)
            for t in range(NT - 3, NT):
                inverse_dev(t, t % 2)

        @block.vector
        def _(dve):
            step = [0]

            def restart():
                dve.sem_clear(dve_step)
                step[0] = 0

            def then(ins):
                step[0] += 1
                ins.then_inc(dve_step, 1)
                dve.wait_ge(dve_step, step[0])

            dve.wait_ge(consts_in, 48)
            dve.tensor_copy(idb[:, :], ident).then_inc(consts_ready, 1)
            dve.tensor_copy(idr[:, :], ident).then_inc(consts_ready, 1)
            dve.tensor_copy(packw[:, :], cf_sb[:, C_PACK:C_PACK + G]).then_inc(consts_ready, 1)

            def normalise(m, k):
                dve.wait_ge(r_ready, m + 1)
                wait(dve, unitT_done, m - 1)
                dve.tensor_scalar(unit[:, k % 2, :], tab[:, k % RING, 0:D], tab[:, k % RING, RN:RN + 1], None, ALU.mult).then_inc(unit_ready, 1)

            def project(i):
                for k in range(P0):
                    m = P0 * i + k
                    dve.wait_ge(wh_done, m + 1)
                    wait(dve, tab_stored[k % RING], 16 * (2 * i + k // RING))
                    dve.tensor_copy(tab[:, k % RING, 0:D], s_ps[k % 2][:, 0:D]).then_inc(tab_copied, 1)
                    if k >= 1:
                        normalise(m - 1, k - 1)
                normalise(P0 * i + P0 - 1, P0 - 1)

            project(0)
            with dve.Fori(1, P0) as i:
                project(i)

            def select_round(a, r):
                dve.max(topb[:, :], base[:, :])
                for g in range(G):
                    last = dve.max(topk[:, g, :], keys[:, g, :])
                then(last)
                dve.tensor_scalar(rows[:, a, bass.ds(r * RND, RND)], topb[:, :], -1.0 / 512, cf_sb[:, C_LANE:C_LANE + 1], ALU.mult, ALU.add)
                then(dve.tensor_copy(topi[:, :, :], topk[:, :, :]))
                then(dve.tensor_tensor(bits[:, :, :, :],
                                       topi[:, :, :].rearrange("p g (s o) -> p s g o", o=1).broadcast_to([P, RND, G, BITS]),
                                       ci_sb[:, I_BIT:I_BIT + BITS].rearrange("p (u v k) -> p u v k", u=1, v=1).broadcast_to([P, RND, G, BITS]),
                                       ALU.bitwise_and))
                then(dve.tensor_scalar(bias[:, a, bass.ds(r * RND * P, RND * P)], bits[:, :, :, :].rearrange("p s g k -> p (s g k)"),
                                       0.0, MASKED, ALU.is_equal, ALU.mult))

            def select(t, a):
                restart()
                dve.wait_ge(packed, NQ * t + NQ)
                then(dve.tensor_copy(words[:, :, :], words_ps[a][:, :].rearrange("p (b g) -> p g b", g=G)))
                own = words[:, :, bass.ds(t, 1)].rearrange("p g o -> p (g o)")
                then(dve.tensor_tensor(own, own, ci_sb[:, I_DIAG:I_DIAG + G], ALU.bitwise_or))
                then(dve.tensor_reduce(used[:, :], words[:, :, :].rearrange("p g b -> p b g"), AX.X, ALU.max))
                then(dve.tensor_scalar(base[:, :], used[:, :], 0.0, None, ALU.is_gt))
                then(dve.tensor_reduce(count[:, :], base[:, :], AX.X, ALU.add))
                dve.sem_inc(count_ready, 1)
                then(dve.tensor_tensor(base[:, :], base[:, :], cf_sb[:, C_BLK:C_BLK + NT], ALU.mult))
                wait(dve, tile_done, t - 1)
                then(dve.tensor_tensor(keys[:, :, :], words[:, :, :], base[:, :].rearrange("p (o b) -> p o b", o=1).broadcast_to([P, G, NT]), ALU.add))
                select_round(a, 0)
                dve.wait_ge(countT_done, t + 1)
                then(dve.tensor_reduce(most[0:1, a:a + 1], words_ps[a][0:1, 0:P], AX.X, ALU.max))
                top = dve.value_load(most[0:1, a:a + 1], min_val=1, max_val=NT)
                with dve.If(top > RND):
                    with dve.Fori(1, (top + (RND - 1)) >> 3) as r:
                        r = round_of(r)
                        restart()
                        then(dve.scalar_tensor_tensor(keys[:, :, :], base[:, :].rearrange("p (o b) -> p o b", o=1).broadcast_to([P, G, NT]),
                                                      topb[:, RND - 1:RND], keys[:, :, :], ALU.is_lt, ALU.mult))
                        then(dve.scalar_tensor_tensor(base[:, :], base[:, :], topb[:, RND - 1:RND], base[:, :], ALU.is_lt, ALU.mult))
                        select_round(a, r)
                dve.sem_inc(sel_done, 1)

            def residual(t, a):
                restart()
                wait(dve, z_ready, t - 1)
                dve.wait_ge(tile_done, t + 1)
                dve.wait_ge(res_in[a], 16 * (half(t) + 1))
                then(dve.reciprocal(den[:, a:a + 1], o_ps[a][:, ONE:ONE + 1]))
                then(dve.scalar_tensor_tensor(y_sb[:, a, :], o_ps[a][:, 0:D], den[:, a:a + 1], x_sb[:, a, :], ALU.mult, ALU.add))
                dve.sem_inc(y_read, 1)
                then(dve.bn_stats(stats[:, :], y_sb[:, a, :]))
                dve.bn_aggr(mv[:, a, :], stats[:, :]).then_inc(var_ready, 1)

            def scale_rows(t, a):
                dve.wait_ge(rstd_ready, t + 1)
                wait(dve, stored[a], 16 * half(t))
                dve.tensor_scalar(z_sb[:, a, :], y_sb[:, a, :], mv[:, a, 0:1], rstd[:, a, 1:2], ALU.subtract, ALU.mult).then_inc(z_ready, 1)

            def tile(t, a):
                for q in range(NQ):
                    dve.wait_ge(adj_in[a][q], 16 * (half(t) + 1))
                    wait(dve, packed, NQ * t + q + 1 - NQ)
                    dve.tensor_scalar(mask[:, q, :], adj_sb[:, a, q, :], 0, None, ALU.is_gt).then_inc(conv_done, 1)
                select(t, a)
                if not isinstance(t, int) or t >= 4:
                    scale_rows(t - 4, a)
                if not isinstance(t, int) or t >= 2:
                    residual(t - 2, a)

            for t in range(4):
                tile(t, t % 2)
            with dve.Fori(2, NT // 2) as i:
                tile(2 * i, 0)
                tile(2 * i + 1, 1)
            for t in range(NT, NT + 4):
                scale_rows(t - 4, t % 2)
                if t < NT + 2:
                    residual(t - 2, t % 2)

        @block.scalar
        def _(act):
            def save_unitT(m, k):
                act.wait_ge(unitT_done, m + 1)
                act.activation(whT[:, :, bass.ds(m * P, P)], gT_ps[k % 2][:, 0:D].rearrange("p (k n) -> p k n", k=KD), ACT.Copy).then_inc(unitT_saved, 1)

            def project(i):
                for k in range(P0):
                    m = P0 * i + k
                    act.wait_ge(tab_copied, m + 1)
                    wait(act, ss_ready, m)
                    act.activation(junk, tab[:, k % RING, 0:D], ACT.Square, accum_out=ssq[:, k:k + 1]).then_inc(ss_ready, 1)
                    if k >= 1:
                        save_unitT(m - 1, k - 1)
                save_unitT(P0 * i + P0 - 1, P0 - 1)

            project(0)
            with act.Fori(1, P0) as i:
                project(i)
            act.wait_ge(ss_ready, NT)

            pair = act.alloc_register("pair")
            act.reg_mov(pair, 1)
            tile_no = act.alloc_register("tile_no")
            act.reg_mov(tile_no, 1)
            act.activation(junk[0:1, 0:1], junk[0:1, 0:1], ACT.Copy).then_inc(prob_ready, 1)
            act.wait_ge(prob_ready, 1)

            def save_gT(b):
                act.wait_ge(gT_done, act.snap(pair))
                act.activation(gT[:, b % 2, :, :, :].rearrange("p k s n -> p (k s n)"), gT_ps[b % 2][:, :], ACT.Copy).then_inc(gT_saved, 1)

            def exps(b):
                act.wait_ge(s_done, act.snap(pair))
                for s in range(2):
                    last = act.activation(prob[:, b % 2, s, :], s_ps[b % 2][:, s * P:(s + 1) * P], ACT.Exp, scale=gat[:, 2 * b + s, RN:RN + 1])
                last.then_inc(prob_ready, 1)

            def tile(t, a):
                pairs = pairs_of(act, a, tile_no)
                with act.Fori(0, (pairs + (PAIRS - 1)) >> 2) as r:
                    with act.If(r > 0):
                        save_gT(0)
                        exps(PAIRS - 1)
                    with act.Else():
                        save_gT(0)
                    act.reg_add(pair, pair, 1)
                    for b in range(1, PAIRS):
                        with act.If(r * PAIRS + b < pairs):
                            save_gT(b)
                            exps(b - 1)
                            act.reg_add(pair, pair, 1)
                for b in range(PAIRS):
                    with act.If(((pairs + (PAIRS - 1)) & (PAIRS - 1)) == b):
                        exps(b)

            for t in range(2):
                tile(t, t % 2)
            with act.Fori(1, NT // 2) as i:
                tile(2 * i, 0)
                tile(2 * i + 1, 1)

        @block.tensor
        def _(pe):
            pe.wait_ge(consts_in, 48)
            pe.wait_ge(consts_ready, 5)

            def unitT(m, k):
                pe.wait_ge(unit_ready, m + 1)
                wait(pe, unitT_saved, m - 1)
                for h in range(KD):
                    last = pe.transpose(gT_ps[k % 2][:, h * P:(h + 1) * P], unit[:, k % 2, h * P:(h + 1) * P], ident)
                last.then_inc(unitT_done, 1)

            def project(i):
                for k in range(P0):
                    m = P0 * i + k
                    pe.wait_ge(x_in[k % RING], 16 * (2 * i + k // RING + 1))
                    wait(pe, tab_copied, m - 1)
                    for h in range(KD):
                        last = pe.matmul(s_ps[k % 2][:, 0:D], x_ring[:, k % RING, h, :], wT_sb[:, h, :], start=(h == 0), stop=(h == KD - 1))
                    last.then_inc(wh_done, 1)
                    if k >= 1:
                        unitT(m - 1, k - 1)
                unitT(P0 * i + P0 - 1, P0 - 1)

            project(0)
            with pe.Fori(1, P0) as i:
                project(i)
            pe.wait_ge(unitT_saved, NT)

            for b in range(PAIRS):
                pe.matmul(o_ps[0][:, b:b + 1], zeros[:, :], zeros[:, 0:1], start=True, stop=True).then_inc(g_free[b], 1)
            pe.matmul(o_ps[0][:, 4:5], zeros[:, :], zeros[:, 0:1], start=True, stop=True).then_inc(s_done, 1)

            pair = pe.alloc_register("pair")
            landed = [pe.alloc_register(f"landed{b}") for b in range(PAIRS)]
            pe.reg_mov(pair, 0)
            tile_no = pe.alloc_register("tile_no")
            pe.reg_mov(tile_no, 1)
            for u in landed:
                pe.reg_mov(u, 32)

            def transposes(b):
                pe.wait_ge(g_ready[b], pe.snap(landed[b]))
                for s in range(2):
                    for h in range(KD):
                        last = pe.transpose(gT_ps[b % 2][:, (2 * h + s) * P:(2 * h + s + 1) * P].bitcast(F32R),
                                            gat[:, 2 * b + s, h * P:(h + 1) * P].bitcast(F32R), idr[:, :])
                last.then_inc(gT_done, 1)
                pe.reg_add(landed[b], landed[b], 32)

            def products(t, a, r, b, n):
                pe.wait_ge(gT_saved, n)
                ps = s_ps[b % 2]
                pe.matmul(ps[:, 0:2 * P], idb[:, :], bias[:, a, bass.ds((r * RND + 2 * b) * P, 2 * P)], start=True, stop=False, skip_group_check=True)
                for s in range(2):
                    for h in range(KD):
                        last = pe.matmul(ps[:, s * P:(s + 1) * P], gT[:, b % 2, h, s, :], whT[:, h, bass.ds(t * P, P)],
                                         start=False, stop=(h == KD - 1), skip_group_check=True)
                last.then_inc(s_done, 1)

            def add_up(a, b, n):
                pe.wait_ge(prob_ready, n)
                for s in range(2):
                    last = pe.matmul(o_ps[a][:, 0:D + 1], prob[:, b % 2, s, :], gat[:, 2 * b + s, 0:D + 1], start=False, stop=False, skip_group_check=True)
                last.then_inc(g_free[b], 1)

            def attend(t, a):
                wait(pe, y_read, t - 1)
                pe.matmul(o_ps[a][:, 0:D + 2], zeros[:, :], zeros[:, 0:1].broadcast_to([P, D + 2]), start=True, stop=False, skip_group_check=True)
                pairs = pairs_of(pe, a, tile_no)
                with pe.Fori(0, (pairs + (PAIRS - 1)) >> 2) as r:
                    r = round_of(r)
                    with pe.If(r > 0):
                        products(t, a, round_of(r - 1), PAIRS - 1, pe.snap(pair))
                        transposes(0)
                        add_up(a, PAIRS - 2, pe.snap(pair))
                    with pe.Else():
                        transposes(0)
                    pe.reg_add(pair, pair, 1)
                    with pe.If(r * PAIRS + 1 < pairs):
                        with pe.If(r > 0):
                            products(t, a, r, 0, pe.snap(pair))
                            transposes(1)
                            add_up(a, PAIRS - 1, pe.snap(pair))
                        with pe.Else():
                            products(t, a, r, 0, pe.snap(pair))
                            transposes(1)
                        pe.reg_add(pair, pair, 1)
                    for b in range(2, PAIRS):
                        with pe.If(r * PAIRS + b < pairs):
                            products(t, a, r, b - 1, pe.snap(pair))
                            transposes(b)
                            add_up(a, b - 2, pe.snap(pair))
                            pe.reg_add(pair, pair, 1)
                last_r = round_of((pairs - 1) >> 2)
                for b in range(PAIRS):
                    with pe.If(((pairs + (PAIRS - 1)) & (PAIRS - 1)) == b):
                        products(t, a, last_r, b, pe.snap(pair))
                        if b >= 1:
                            add_up(a, b - 1, pe.snap(pair))
                        else:
                            with pe.If(pairs > 1):
                                add_up(a, PAIRS - 1, pe.snap(pair))
                        add_up(a, b, pe.snap(pair) + 1)
                pe.matmul(o_ps[a][:, D:D + 2], zeros[:, :], zeros[:, 0:2], start=False, stop=True, skip_group_check=True).then_inc(tile_done, 1)

            def tile(t, a):
                for q in range(NQ):
                    pe.wait_ge(conv_done, NQ * t + q + 1)
                    for b in range(QB):
                        at = (q * QB + b) * G
                        last = pe.matmul(words_ps[a][:, at:at + G], mask[:, q, b * P:(b + 1) * P], packw[:, :], start=True, stop=True)
                    last.then_inc(packed, 1)
                pe.wait_ge(count_ready, t + 1)
                pe.matmul(words_ps[a][0:1, 0:P], count[:, :], ident, start=True, stop=True).then_inc(countT_done, 1)
                if not isinstance(t, int) or t >= 1:
                    attend(t - 1, 1 - a)

            tiles(pe, tile)
            attend(NT - 1, (NT - 1) % 2)


def kernel(x, adj, L0_gnn_W):
    from concourse import bacc
    from concourse.bass_utils import run_bass_kernel_spmd

    cf = np.zeros((P, C_F), np.float32)
    lane = np.arange(P)
    cf[:, C_ID:C_ID + P] = np.eye(P)
    cf[:, C_BLK:C_BLK + NT] = (NT - np.arange(NT)) * 65536.0
    cf[lane, C_PACK + lane // BITS] = 2.0 ** (lane % BITS)
    cf[:, C_LANE] = N + lane
    cf[:, C_HALF], cf[:, C_TINY], cf[:, C_EPS] = -0.5, TINY, EPS_LN
    ci = np.zeros((P, I_N), np.int32)
    ci[:, I_BIT:I_BIT + BITS] = 1 << np.arange(BITS)
    ci[lane, I_DIAG + lane // BITS] = 1 << (lane % BITS)

    x, adj, w = np.asarray(x), np.asarray(adj), np.asarray(L0_gnn_W)
    arrays = {
        "xT": np.ascontiguousarray(x.reshape(NT, P, KD, P).transpose(0, 3, 2, 1)),
        "x": np.ascontiguousarray(x),
        "adj": np.ascontiguousarray(adj),
        "wT": np.ascontiguousarray(w.T),
        "cf": cf,
        "ci": ci,
    }
    nc = bacc.Bacc("TRN2", target_bir_lowering=False, num_devices=1)
    args = [nc.dram_tensor(n, a.shape, mybir.dt.from_np(a.dtype), kind="ExternalInput").ap() for n, a in arrays.items()]
    out = nc.dram_tensor("out", (N, D), F32, kind="ExternalOutput").ap()
    build(nc, *args, out)
    return run_bass_kernel_spmd(nc, [arrays], core_ids=[0]).results[0]["out"]
```

```python
from contextlib import ExitStack

import numpy as np
import concourse.bass as bass
from concourse import mybir

F32 = mybir.dt.float32
F32R = mybir.dt.float32r
BF16 = mybir.dt.bfloat16
I32 = mybir.dt.int32
U32 = mybir.dt.uint32
ALU = mybir.AluOpType
ACT = mybir.ActivationFunctionType
AX = mybir.AxisListType

P = 128
N = 8192
D = 256
KD = D // P
NT = N // P
NQ = 8
QC = N // NQ
QB = QC // P
BITS = 16
G = P // BITS
RND = 8
PAIRS = 8
TW = D + 2
ONE, RN = D, D + 1
P0 = 8
XR = 4
RING = 8
EPS_LN = 1e-5
TINY = 1e-36
MASKED = -3e38

C_ID, C_BLK, C_PACK, C_LANE = 0, P, P + NT, P + NT + G
C_HALF, C_TINY, C_EPS, C_F = C_LANE + 1, C_LANE + 2, C_LANE + 3, C_LANE + 4
I_BIT, I_DIAG, I_N = 0, BITS, BITS + G


def build(nc, xT, x, adj, wT, cf, ci, out):
    table = nc.dram_tensor("table", (N, TW), F32).ap()
    ctx = ExitStack()
    with ctx:
        def sb(name, shape, dt):
            return ctx.enter_context(nc.sbuf_tensor(name, shape, dt))

        def sem(name):
            return ctx.enter_context(nc.semaphore(name))

        whT = sb("whT", [P, KD, N], F32)
        adj_sb = sb("adj_sb", [P, 2 * NQ - 1, QC], I32)
        mask = sb("mask", [P, NQ, QC], BF16)
        bias = sb("bias", [P, 2, N], BF16)
        gat = sb("gat", [P, PAIRS, 2, TW], F32)
        gT = sb("gT", [P, 2, KD, 2, P], F32)
        prob = sb("prob", [P, 2, 2, P], F32)
        own = sb("own", [P, G], I32)
        keys = sb("keys", [P, G, NT], F32)
        base = sb("base", [P, NT], F32)
        used = sb("used", [P, NT], F32)
        small = sb("small", [P, 3], F32)
        most = sb("most", [1, 2], I32)
        topb = sb("topb", [P, RND], F32)
        topk = sb("topk", [P, G, RND], F32)
        topi = sb("topi", [P, G, RND], I32)
        bits = sb("bits", [P, RND, G, BITS], I32)
        rows = sb("rows", [P, 2, NT], U32)
        rows_now = sb("rows_now", [P, PAIRS, 2], U32)
        xyz = sb("xyz", [P, 4, D], F32)
        stats = sb("stats", [P, 6], F32)
        mv = sb("mv", [P, 2, 2], F32)
        rstd = sb("rstd", [P, 2, 2], F32)
        cf_sb = sb("cf_sb", [P, C_F], F32)
        ci_sb = sb("ci_sb", [P, I_N], I32)
        idb = sb("idb", [P, P], BF16)
        idr = sb("idr", [P, P], F32R)
        packw = sb("packw", [P, G], BF16)
        zeros = sb("zeros", [P, P], BF16)

        wT_sb = mask[:, :, :].rearrange("p q c -> p (q c)").bitcast(F32)[:, 0:KD * D].rearrange("p (k o) -> p k o", k=KD)
        den, count = small[:, 0:2], small[:, 2:3]
        ident = cf_sb[:, C_ID:C_ID + P]
        x_ring = xyz[:, :, :].rearrange("p r (k n) -> p r k n", k=KD)
        unit = prob[:, :, :, :].rearrange("p a b c -> p a (b c)")
        tab = bias[:, 1, :].bitcast(F32)[:, 0:RING * TW].rearrange("p (r w) -> p r w", r=RING)
        junk = gT[:, 0, 0, :, :].rearrange("p b c -> p (b c)")
        ssq, ssg = gT[:, 1, 0, 0, 0:P0], gT[:, 1, 0, 0, P0:2 * P0]

        def bank(name):
            return ctx.enter_context(nc.psum_tensor(name, [P, 512], F32))

        words_ps = [bank("words0"), bank("words1")]
        gT_ps = [bank("gT0"), bank("gT1")]
        s_ps = [bank("s0"), bank("s1")]
        o_ps = [bank("o0"), bank("o1")]

        consts_in = sem("consts_in")
        consts_ready = sem("consts_ready")
        x_in = [sem(f"x_in{k}") for k in range(XR // 2)]
        wh_done = sem("wh_done")
        tab_copied = sem("tab_copied")
        ss_ready = sem("ss_ready")
        r_ready = sem("r_ready")
        unit_ready = sem("unit_ready")
        unitT_done = sem("unitT_done")
        unitT_saved = sem("unitT_saved")
        tab_stored = [sem(f"tab_stored{k}") for k in range(RING // 2)]
        table_ready = sem("table_ready")
        adj_in = [[sem(f"adj_in{a}{q}") for q in range(NQ)] for a in range(2)]
        conv_done = sem("conv_done")
        packed = sem("packed")
        count_ready = sem("count_ready")
        words_read = sem("words_read")
        countT_done = sem("countT_done")
        sel_done = sem("sel_done")
        g_ready = [sem(f"g_ready{k}") for k in range(PAIRS)]
        g_free = [sem(f"g_free{k}") for k in range(PAIRS)]
        gT_done = sem("gT_done")
        gT_saved = sem("gT_saved")
        s_done = sem("s_done")
        prob_ready = sem("prob_ready")
        tile_done = sem("tile_done")
        res_in = [sem("res_in0"), sem("res_in1")]
        y_read = sem("y_read")
        var_ready = sem("var_ready")
        rstd_ready = sem("rstd_ready")
        z_ready = sem("z_ready")
        stored = [sem("stored0"), sem("stored1")]
        dve_step = sem("dve_step")
        pool_step = sem("pool_step")

        def pairs_of(eng, a, tile_no):
            selected = eng.snap(tile_no)
            eng.wait_ge(consts_in, 48)
            eng.wait_ge(sel_done, selected)
            top = eng.value_load(most[0:1, a:a + 1], min_val=1, max_val=NT)
            eng.reg_add(tile_no, tile_no, 1)
            return eng.snap((top + 1) >> 1)

        def wait(eng, s, value):
            if not isinstance(value, int) or value > 0:
                eng.wait_ge(s, value)

        def tiles(eng, body):
            for t in range(3):
                body(t, t % 2)
            with eng.Fori(0, (NT - 6) // 2) as i:
                body(2 * i + 3, 1)
                body(2 * i + 4, 0)
            for t in range(NT - 3, NT):
                body(t, t % 2)

        def buffer(a, b):
            return (b + a * PAIRS // 2) % PAIRS

        def pass_of(r):
            return nc.s_assert_within(r, 0, NT // (2 * PAIRS) - 1, skip_runtime_bounds_check_because="a lane has 64 columns")

        def ring(t):
            return xyz[:, t % 4, :] if isinstance(t, int) else xyz[:, bass.ds(t & 3, 1), :].rearrange("p r d -> p (r d)")

        def adj_part(a, q):
            return adj_sb[:, 2 * NQ - 2 if q == NQ - 1 else a * (NQ - 1) + q, :]

        def half(t):
            return t // 2 if isinstance(t, int) else (t >> 1)

        block = ctx.enter_context(nc.Block())

        @block.sync
        def _(sp):
            sp.dma_start(cf_sb[:, :], cf).then_inc(consts_in, 16)
            sp.dma_start(ci_sb[:, :], ci).then_inc(consts_in, 16)
            sp.dma_start(wT_sb[:, :, :], wT.rearrange("(k p) o -> p k o", p=P)).then_inc(consts_in, 16)

            def load_adj(t, a, q):
                used = NQ * t + q + 1 - (NQ if q == NQ - 1 else 2 * NQ)
                before = 16 * (half(t) + (1 if q >= 2 else a))
                if not isinstance(t, int):
                    used, before = sp.snap(used), sp.snap(before)
                    sp.wait_ge(consts_in, 48)
                wait(sp, conv_done, used)
                if not isinstance(t, int) or t >= 2:
                    sp.wait_ge(adj_in[a if q >= 2 else 1 - a][(q - 2) % NQ], before)
                sp.dma_start(adj_part(a, q), adj[bass.ds(t * P, P), q * QC:(q + 1) * QC]).then_inc(adj_in[a][q], 16)

            def project(i, load):
                for k in range(0, P0, 2):
                    m = P0 * i + k
                    wait(sp, wh_done, m - 2)
                    sp.dma_start(x_ring[:, k % XR:k % XR + 2, :, :].rearrange("p a k n -> p a (k n)"),
                                 xT[m:m + 2, :, :, :].rearrange("a p k n -> p a (k n)")).then_inc(x_in[k % XR // 2], 16)
                    if m >= 4:
                        store(m - 4)
                    if k % 4 == 2 and m < NT - 2:
                        load(k // 4)

            def store(m):
                sp.wait_ge(r_ready, m + 2)
                k = m % RING
                sp.dma_start(table[m * P:(m + 2) * P, :].rearrange("(a p) w -> p a w", p=P), tab[:, k:k + 2, :]).then_inc(tab_stored[k // 2], 16)

            for i in range(P0):
                project(i, lambda h: load_adj(i // 4, i // 4, i % 4 * 2 + h))
            for m in (NT - 4, NT - 2):
                store(m)
            for k in range(RING // 2):
                sp.wait_ge(tab_stored[k], 16 * NT // RING)
            sp.sem_inc(table_ready, 1)

            place = sp.alloc_register("place")

            def load_res(t, a):
                gone = 16 * half(t - 2)
                if isinstance(t, int):
                    to = ring(t)
                else:
                    sp.reg_mov(place, t & 3)
                    at = nc.s_assert_within(sp.snap(place), 0, 3, skip_runtime_bounds_check_because="two bits")
                    to = xyz[:, bass.ds(at, 1), :].rearrange("p r d -> p (r d)")
                wait(sp, y_read, t - 1)
                if not isinstance(t, int) or t >= 4:
                    sp.wait_ge(stored[a], gone)
                sp.dma_start(to, x[bass.ds(t * P, P), :]).then_inc(res_in[a], 16)

            def store_out(t, a):
                sp.wait_ge(z_ready, t + 1)
                sp.dma_start(out[bass.ds(t * P, P), :], ring(t)).then_inc(stored[a], 16)

            load_adj(1, 1, NQ - 1)
            for t in range(2, 8):
                for q in range(NQ):
                    load_adj(t, t % 2, q)
                if t >= 4:
                    load_res(t - 4, t % 2)
            with sp.Fori(4, NT // 2) as i:
                for a in range(2):
                    store_out(2 * i + a - 8, a)
                    for q in range(NQ):
                        load_adj(2 * i + a, a, q)
                    load_res(2 * i + a - 4, a)
            for t in range(NT, NT + 8):
                store_out(t - 8, t % 2)
                if t < NT + 4:
                    load_res(t - 4, t % 2)
            for a in range(2):
                sp.wait_ge(stored[a], 16 * NT // 2)

        @block.gpsimd
        def _(pool):
            pool.memset(gat[:, :, :, :], 0.0).then_inc(consts_ready, 1)
            pool.memset(tab[:, :, ONE:ONE + 1], 1.0).then_inc(pool_step, 1)
            pool.memset(zeros[:, :], 0.0).then_inc(consts_ready, 1)

            def project(i):
                for k in range(P0):
                    m = P0 * i + k
                    pool.sem_clear(pool_step)
                    pool.wait_ge(ss_ready, m + 1)
                    pool.tensor_tensor(ssg[:, k:k + 1], ssq[:, k:k + 1], cf_sb[:, C_TINY:C_TINY + 1], ALU.add).then_inc(pool_step, 1)
                    pool.wait_ge(pool_step, 1)
                    pool.tensor_tensor(tab[:, k % RING, RN:RN + 1], ssg[:, k:k + 1], cf_sb[:, C_HALF:C_HALF + 1], ALU.pow).then_inc(r_ready, 1)

            pool.wait_ge(pool_step, 1)
            pool.wait_ge(consts_in, 48)
            project(0)
            with pool.Fori(1, P0) as i:
                project(i)

            pool.wait_ge(table_ready, 1)
            tile_no = pool.alloc_register("tile_no")
            pool.reg_mov(tile_no, 1)
            uses = [pool.alloc_register(f"uses{k}") for k in range(PAIRS)]
            for u in uses:
                pool.reg_mov(u, 1)

            def gather(a, r, b):
                k = buffer(a, b)
                pool.sem_clear(pool_step)
                pool.wait_ge(g_free[k], pool.snap(uses[k]))
                pool.tensor_copy(rows_now[:, k, :], rows[:, a, bass.ds((r * PAIRS + b) * 2, 2)]).then_inc(pool_step, 1)
                pool.wait_ge(pool_step, 1)
                for s in range(2):
                    pool.indirect_dma_start(
                        out=gat[:, k, s, :], out_offset=None, in_=table,
                        in_offset=bass.IndirectOffsetOnAxis(ap=rows_now[:, k, s:s + 1], axis=0),
                        bounds_check=N - 1, oob_is_err=False).then_inc(g_ready[k], 16)
                pool.reg_add(uses[k], uses[k], 1)

            def inverse_dev(t, a):
                pool.sem_clear(pool_step)
                pool.wait_ge(var_ready, t + 1)
                pool.tensor_tensor(rstd[:, a, 0:1], mv[:, a, 1:2], cf_sb[:, C_EPS:C_EPS + 1], ALU.add).then_inc(pool_step, 1)
                pool.wait_ge(pool_step, 1)
                pool.tensor_tensor(rstd[:, a, 1:2], rstd[:, a, 0:1], cf_sb[:, C_HALF:C_HALF + 1], ALU.pow).then_inc(rstd_ready, 1)

            def tile(t, a):
                if not isinstance(t, int) or t >= 3:
                    inverse_dev(t - 3, 1 - a)
                pairs = pairs_of(pool, a, tile_no)

                def step(r, b):
                    with pool.If(r * PAIRS + b < pairs):
                        gather(a, r, b)
                        if b + 1 < PAIRS:
                            step(r, b + 1)

                with pool.Fori(0, (pairs + (PAIRS - 1)) >> 3) as r:
                    r = pass_of(r)
                    gather(a, r, 0)
                    step(r, 1)

            tiles(pool, tile)
            for t in range(NT - 3, NT):
                inverse_dev(t, t % 2)

        @block.vector
        def _(dve):
            step = [0]

            def restart():
                dve.sem_clear(dve_step)
                step[0] = 0

            def then(ins):
                step[0] += 1
                ins.then_inc(dve_step, 1)
                dve.wait_ge(dve_step, step[0])

            dve.wait_ge(consts_in, 48)
            dve.tensor_copy(idb[:, :], ident).then_inc(consts_ready, 1)
            dve.tensor_copy(idr[:, :], ident).then_inc(consts_ready, 1)
            dve.tensor_copy(packw[:, :], cf_sb[:, C_PACK:C_PACK + G]).then_inc(consts_ready, 1)

            def normalise(m, k):
                dve.wait_ge(r_ready, m + 1)
                wait(dve, unitT_done, m - 1)
                dve.tensor_scalar(unit[:, k % 2, :], tab[:, k, 0:D], tab[:, k, RN:RN + 1], None, ALU.mult).then_inc(unit_ready, 1)

            def project(i):
                for k in range(P0):
                    m = P0 * i + k
                    dve.wait_ge(wh_done, m + 1)
                    wait(dve, tab_stored[k // 2], 16 * i)
                    dve.tensor_copy(tab[:, k, 0:D], s_ps[k % 2][:, 0:D]).then_inc(tab_copied, 1)
                    if not isinstance(m, int) or m >= 2:
                        normalise(m - 2, (k - 2) % P0)

            project(0)
            with dve.Fori(1, P0) as i:
                project(i)
            for m in range(NT - 2, NT):
                normalise(m, m % P0)

            def select_round(a, r):
                dve.max(topb[:, :], base[:, :])
                for g in range(G):
                    last = dve.max(topk[:, g, :], keys[:, g, :])
                then(last)
                dve.tensor_scalar(rows[:, a, bass.ds(r * RND, RND)], topb[:, :], -1.0 / 512, cf_sb[:, C_LANE:C_LANE + 1], ALU.mult, ALU.add)
                then(dve.tensor_copy(topi[:, :, :], topk[:, :, :]))
                then(dve.tensor_tensor(bits[:, :, :, :],
                                       topi[:, :, :].rearrange("p g (s o) -> p s g o", o=1).broadcast_to([P, RND, G, BITS]),
                                       ci_sb[:, I_BIT:I_BIT + BITS].rearrange("p (u v k) -> p u v k", u=1, v=1).broadcast_to([P, RND, G, BITS]),
                                       ALU.bitwise_and))
                then(dve.tensor_scalar(bias[:, a, bass.ds(r * RND * P, RND * P)], bits[:, :, :, :].rearrange("p s g k -> p (s g k)"),
                                       0.0, MASKED, ALU.is_equal, ALU.mult))

            def convert(t, a):
                for q in range(NQ):
                    dve.wait_ge(adj_in[a][q], 16 * (half(t) + 1))
                    wait(dve, packed, NQ * t + q + 1 - NQ)
                    dve.tensor_scalar(mask[:, q, :], adj_part(a, q), 0, None, ALU.is_gt).then_inc(conv_done, 1)

            def make_keys(t, a):
                restart()
                dve.wait_ge(packed, NQ * t + NQ)
                by_block = words_ps[a][:, :].rearrange("p (b g) -> p b g", g=G)
                dve.tensor_copy(own[:, :], words_ps[a][:, bass.ds(t * G, G)])
                then(dve.tensor_reduce(used[:, :], by_block, AX.X, ALU.max))
                here = used[:, bass.ds(t, 1)]
                dve.tensor_tensor(own[:, :], own[:, :], ci_sb[:, I_DIAG:I_DIAG + G], ALU.bitwise_or)
                then(dve.tensor_scalar(here, here, 1.0, None, ALU.add))
                then(dve.tensor_scalar(base[:, :], used[:, :], 0.0, None, ALU.is_gt))
                dve.tensor_reduce(count[:, :], base[:, :], AX.X, ALU.add).then_inc(count_ready, 1)
                then(dve.tensor_tensor(base[:, :], base[:, :], cf_sb[:, C_BLK:C_BLK + NT], ALU.mult))
                then(dve.tensor_tensor(keys[:, :, :], words_ps[a][:, :].rearrange("p (b g) -> p g b", g=G),
                                       base[:, :].rearrange("p (o b) -> p o b", o=1).broadcast_to([P, G, NT]), ALU.add))
                dve.sem_inc(words_read, 1)
                then(dve.tensor_scalar(keys[:, :, bass.ds(t, 1)].rearrange("p g o -> p (g o)"), own[:, :], base[:, bass.ds(t, 1)], None, ALU.add))

            def select(t, a):
                restart()
                if isinstance(t, int) and t == 1:
                    dve.wait_ge(table_ready, 1)
                wait(dve, tile_done, t - 1)
                dve.wait_ge(countT_done, t + 1)
                dve.tensor_reduce(most[0:1, a:a + 1], words_ps[a][0:1, 0:P], AX.X, ALU.max).then_inc(dve_step, 1)
                step[0] += 1
                select_round(a, 0)
                top = dve.value_load(most[0:1, a:a + 1], min_val=1, max_val=NT)
                with dve.If(top > RND):
                    with dve.Fori(1, (top + (RND - 1)) >> 3) as r:
                        r = nc.s_assert_within(r, 1, NT // RND - 1, skip_runtime_bounds_check_because="a lane has 64 columns")
                        restart()
                        then(dve.scalar_tensor_tensor(keys[:, :, :], base[:, :].rearrange("p (o b) -> p o b", o=1).broadcast_to([P, G, NT]),
                                                      topb[:, RND - 1:RND], keys[:, :, :], ALU.is_lt, ALU.mult))
                        then(dve.scalar_tensor_tensor(base[:, :], base[:, :], topb[:, RND - 1:RND], base[:, :], ALU.is_lt, ALU.mult))
                        select_round(a, r)
                dve.sem_inc(sel_done, 1)

            def residual(t, a):
                restart()
                dve.wait_ge(tile_done, t + 1)
                dve.wait_ge(res_in[a], 16 * (half(t) + 1))
                then(dve.reciprocal(den[:, a:a + 1], o_ps[a][:, ONE:ONE + 1]))
                then(dve.scalar_tensor_tensor(ring(t), o_ps[a][:, 0:D], den[:, a:a + 1], ring(t), ALU.mult, ALU.add))
                dve.sem_inc(y_read, 1)
                then(dve.bn_stats(stats[:, :], ring(t)))
                dve.bn_aggr(mv[:, a, :], stats[:, :]).then_inc(var_ready, 1)

            def scale_rows(t, a):
                dve.wait_ge(rstd_ready, t + 1)
                wait(dve, stored[a], 16 * half(t))
                dve.tensor_scalar(ring(t), ring(t), mv[:, a, 0:1], rstd[:, a, 1:2], ALU.subtract, ALU.mult).then_inc(z_ready, 1)

            def tile(t, a):
                select(t, a)
                if not isinstance(t, int) or t >= 4:
                    scale_rows(t - 4, a)
                if not isinstance(t, int) or t >= 2:
                    residual(t - 2, a)
                if not isinstance(t, int) or t + 1 < NT:
                    make_keys(t + 1, 1 - a)
                if not isinstance(t, int) or t + 2 < NT:
                    convert(t + 2, a)

            convert(0, 0)
            make_keys(0, 0)
            convert(1, 1)
            for t in range(4):
                tile(t, t % 2)
            with dve.Fori(2, NT // 2 - 1) as i:
                tile(2 * i, 0)
                tile(2 * i + 1, 1)
            for t in range(NT - 2, NT):
                tile(t, t % 2)
            for t in range(NT, NT + 4):
                scale_rows(t - 4, t % 2)
                if t < NT + 2:
                    residual(t - 2, t % 2)

        @block.scalar
        def _(act):
            def save_unitT(m, k):
                act.wait_ge(unitT_done, m + 1)
                act.activation(whT[:, :, bass.ds(m * P, P)], gT_ps[k % 2][:, 0:D].rearrange("p (k n) -> p k n", k=KD), ACT.Copy).then_inc(unitT_saved, 1)

            def project(i):
                for k in range(P0):
                    m = P0 * i + k
                    act.wait_ge(tab_copied, m + 1)
                    wait(act, ss_ready, m)
                    wait(act, r_ready, m - P0 + 1)
                    act.activation(junk, tab[:, k, 0:D], ACT.Square, accum_out=ssq[:, k:k + 1]).then_inc(ss_ready, 1)
                    if not isinstance(m, int) or m >= 3:
                        save_unitT(m - 3, (k - 3) % P0)

            project(0)
            with act.Fori(1, P0) as i:
                project(i)
            for m in range(NT - 3, NT):
                save_unitT(m, m % P0)
            act.wait_ge(r_ready, NT)

            pair = act.alloc_register("pair")
            act.reg_mov(pair, 1)
            tile_no = act.alloc_register("tile_no")
            act.reg_mov(tile_no, 1)
            act.activation(junk[0:1, 0:1], junk[0:1, 0:1], ACT.Copy).then_inc(prob_ready, 1)
            act.wait_ge(prob_ready, 1)

            def save_gT(b):
                act.wait_ge(gT_done, act.snap(pair))
                act.activation(gT[:, b % 2, :, :, :].rearrange("p k s n -> p (k s n)"), gT_ps[b % 2][:, :], ACT.Copy).then_inc(gT_saved, 1)

            def exps(a, b):
                act.wait_ge(s_done, act.snap(pair))
                for s in range(2):
                    last = act.activation(prob[:, b % 2, s, :], s_ps[b % 2][:, s * P:(s + 1) * P], ACT.Exp, scale=gat[:, buffer(a, b), s, RN:RN + 1])
                last.then_inc(prob_ready, 1)

            def tile(t, a):
                pairs = pairs_of(act, a, tile_no)

                def step(r, b):
                    with act.If(r * PAIRS + b < pairs):
                        save_gT(b)
                        exps(a, b - 1)
                        act.reg_add(pair, pair, 1)
                        if b + 1 < PAIRS:
                            step(r, b + 1)
                        else:
                            with act.If(r * PAIRS + PAIRS == pairs):
                                exps(a, b)
                    with act.Else():
                        exps(a, b - 1)

                with act.Fori(0, (pairs + (PAIRS - 1)) >> 3) as r:
                    with act.If(r > 0):
                        save_gT(0)
                        exps(a, PAIRS - 1)
                    with act.Else():
                        save_gT(0)
                    act.reg_add(pair, pair, 1)
                    step(r, 1)

            for t in range(2):
                tile(t, t % 2)
            with act.Fori(1, NT // 2) as i:
                tile(2 * i, 0)
                tile(2 * i + 1, 1)

        @block.tensor
        def _(pe):
            pe.wait_ge(consts_in, 48)
            pe.wait_ge(consts_ready, 5)

            def unitT(m, k):
                pe.wait_ge(unit_ready, m + 1)
                wait(pe, unitT_saved, m - 1)
                for h in range(KD):
                    last = pe.transpose(gT_ps[k % 2][:, h * P:(h + 1) * P], unit[:, k % 2, h * P:(h + 1) * P], ident)
                last.then_inc(unitT_done, 1)

            def project(i):
                for k in range(P0):
                    m = P0 * i + k
                    pe.wait_ge(x_in[k % XR // 2], 16 * (2 * i + k // XR + 1))
                    wait(pe, tab_copied, m - 1)
                    for h in range(KD):
                        last = pe.matmul(s_ps[k % 2][:, 0:D], x_ring[:, k % XR, h, :], wT_sb[:, h, :], start=(h == 0), stop=(h == KD - 1))
                    last.then_inc(wh_done, 1)
                    if not isinstance(m, int) or m >= 3:
                        unitT(m - 3, (k - 3) % P0)

            project(0)
            with pe.Fori(1, P0) as i:
                project(i)
            for m in range(NT - 3, NT):
                unitT(m, m % P0)
            pe.wait_ge(unitT_saved, NT)

            for k in range(PAIRS):
                pe.matmul(o_ps[0][:, k:k + 1], zeros[:, :], zeros[:, 0:1], start=True, stop=True).then_inc(g_free[k], 1)
            pe.matmul(o_ps[0][:, PAIRS:PAIRS + 1], zeros[:, :], zeros[:, 0:1], start=True, stop=True).then_inc(s_done, 1)

            pair = pe.alloc_register("pair")
            landed = [pe.alloc_register(f"landed{k}") for k in range(PAIRS)]
            pe.reg_mov(pair, 0)
            tile_no = pe.alloc_register("tile_no")
            pe.reg_mov(tile_no, 1)
            for u in landed:
                pe.reg_mov(u, 32)

            def transposes(a, b):
                k = buffer(a, b)
                pe.wait_ge(g_ready[k], pe.snap(landed[k]))
                for s in range(2):
                    for h in range(KD):
                        last = pe.transpose(gT_ps[b % 2][:, (2 * h + s) * P:(2 * h + s + 1) * P].bitcast(F32R),
                                            gat[:, k, s, h * P:(h + 1) * P].bitcast(F32R), idr[:, :])
                last.then_inc(gT_done, 1)
                pe.reg_add(landed[k], landed[k], 32)

            def products(t, a, r, b, n):
                pe.wait_ge(gT_saved, n)
                ps = s_ps[b % 2]
                pe.matmul(ps[:, 0:2 * P], idb[:, :], bias[:, a, bass.ds((r * PAIRS + b) * 2 * P, 2 * P)], start=True, stop=False, skip_group_check=True)
                for s in range(2):
                    for h in range(KD):
                        last = pe.matmul(ps[:, s * P:(s + 1) * P], gT[:, b % 2, h, s, :], whT[:, h, bass.ds(t * P, P)],
                                         start=False, stop=(h == KD - 1), skip_group_check=True)
                last.then_inc(s_done, 1)

            def add_up(a, b, n):
                pe.wait_ge(prob_ready, n)
                for s in range(2):
                    last = pe.matmul(o_ps[a][:, 0:D + 1], prob[:, b % 2, s, :], gat[:, buffer(a, b), s, 0:D + 1], start=False, stop=False, skip_group_check=True)
                last.then_inc(g_free[buffer(a, b)], 1)

            def attend(t, a, pairs):
                wait(pe, y_read, t - 1)
                pe.matmul(o_ps[a][:, 0:D + 2], zeros[:, :], zeros[:, 0:1].broadcast_to([P, D + 2]), start=True, stop=False, skip_group_check=True)

                def finish(r, b):
                    more = not isinstance(t, int) or t + 1 < NT
                    held = buffer(1 - a, 0) in (buffer(a, b), buffer(a, b - 1))
                    products(t, a, r, b, pe.snap(pair))
                    if more and not held:
                        transposes(1 - a, 0)
                    if b >= 1:
                        add_up(a, b - 1, pe.snap(pair))
                    else:
                        with pe.If(pairs > 1):
                            add_up(a, PAIRS - 1, pe.snap(pair))
                    add_up(a, b, pe.snap(pair) + 1)
                    if more and held:
                        transposes(1 - a, 0)
                    pe.reg_add(pair, pair, 1)

                def step(r, b):
                    with pe.If(r * PAIRS + b < pairs):
                        products(t, a, r, b - 1, pe.snap(pair))
                        transposes(a, b)
                        if b >= 2:
                            add_up(a, b - 2, pe.snap(pair))
                        else:
                            with pe.If(r > 0):
                                add_up(a, PAIRS - 1, pe.snap(pair))
                        pe.reg_add(pair, pair, 1)
                        if b + 1 < PAIRS:
                            step(r, b + 1)
                        else:
                            with pe.If(r * PAIRS + PAIRS == pairs):
                                finish(r, b)
                    with pe.Else():
                        finish(r, b - 1)

                with pe.Fori(0, (pairs + (PAIRS - 1)) >> 3) as r:
                    r = pass_of(r)
                    with pe.If(r > 0):
                        products(t, a, pass_of(r - 1), PAIRS - 1, pe.snap(pair))
                        transposes(a, 0)
                        add_up(a, PAIRS - 2, pe.snap(pair))
                        pe.reg_add(pair, pair, 1)
                    step(r, 1)
                pe.matmul(o_ps[a][:, D:D + 2], zeros[:, :], zeros[:, 0:2], start=False, stop=True, skip_group_check=True).then_inc(tile_done, 1)

            def pack(t, a):
                for q in range(NQ):
                    pe.wait_ge(conv_done, NQ * t + q + 1)
                    for b in range(QB):
                        at = (q * QB + b) * G
                        last = pe.matmul(words_ps[a][:, at:at + G], mask[:, q, b * P:(b + 1) * P], packw[:, :], start=True, stop=True)
                    last.then_inc(packed, 1)

            def transpose_count(t, a):
                pe.wait_ge(count_ready, t + 1)
                pe.wait_ge(words_read, t + 1)
                pe.matmul(words_ps[a][0:1, 0:P], count[:, :], ident, start=True, stop=True).then_inc(countT_done, 1)

            def tile(t, a):
                if not isinstance(t, int) or t + 1 < NT:
                    transpose_count(t + 1, 1 - a)
                pairs = pairs_of(pe, a, tile_no)
                if not isinstance(t, int) or t + 2 < NT:
                    pack(t + 2, a)
                attend(t, a, pairs)

            pack(0, 0)
            transpose_count(0, 0)
            pack(1, 1)
            transposes(0, 0)
            pe.reg_add(pair, pair, 1)
            tiles(pe, tile)


def kernel(x, adj, L0_gnn_W):
    from concourse import bacc
    from concourse.bass_utils import run_bass_kernel_spmd

    cf = np.zeros((P, C_F), np.float32)
    lane = np.arange(P)
    cf[:, C_ID:C_ID + P] = np.eye(P)
    cf[:, C_BLK:C_BLK + NT] = (NT - np.arange(NT)) * 65536.0
    cf[lane, C_PACK + lane // BITS] = 2.0 ** (lane % BITS)
    cf[:, C_LANE] = N + lane
    cf[:, C_HALF], cf[:, C_TINY], cf[:, C_EPS] = -0.5, TINY, EPS_LN
    ci = np.zeros((P, I_N), np.int32)
    ci[:, I_BIT:I_BIT + BITS] = 1 << np.arange(BITS)
    ci[lane, I_DIAG + lane // BITS] = 1 << (lane % BITS)

    x, adj, w = np.asarray(x), np.asarray(adj), np.asarray(L0_gnn_W)
    arrays = {
        "xT": np.ascontiguousarray(x.reshape(NT, P, KD, P).transpose(0, 3, 2, 1)),
        "x": np.ascontiguousarray(x),
        "adj": np.ascontiguousarray(adj),
        "wT": np.ascontiguousarray(w.T),
        "cf": cf,
        "ci": ci,
    }
    nc = bacc.Bacc("TRN2", target_bir_lowering=False, num_devices=1)
    args = [nc.dram_tensor(n, a.shape, mybir.dt.from_np(a.dtype), kind="ExternalInput").ap() for n, a in arrays.items()]
    out = nc.dram_tensor("out", (N, D), F32, kind="ExternalOutput").ap()
    build(nc, *args, out)
    return run_bass_kernel_spmd(nc, [arrays], core_ids=[0]).results[0]["out"]
```

```python
from contextlib import ExitStack

import numpy as np
import concourse.bass as bass
from concourse import mybir

F32 = mybir.dt.float32
F32R = mybir.dt.float32r
BF16 = mybir.dt.bfloat16
I32 = mybir.dt.int32
U32 = mybir.dt.uint32
U16 = mybir.dt.uint16
ALU = mybir.AluOpType
ACT = mybir.ActivationFunctionType
AX = mybir.AxisListType

P = 128
N = 8192
D = 256
KD = D // P
NT = N // P
NQ = 8
QC = N // NQ
QB = QC // P
BITS = 16
G = P // BITS
RND = 8
PAIRS = 8
TW = D + 2
ONE, RN = D, D + 1
P0 = 8
XR = 4
RING = 8
EPS_LN = 1e-5
TINY = 1e-36
EPS_SIM = 1e-8
FAR = 2.0
FLOOR = -3e20
PLENTY = NT * (N // P // 2) + 1
MASKED = -1e30

C_ID, C_BLK, C_PACK, C_LANE = 0, P, P + NT, P + NT + G
C_HALF, C_TINY, C_EPS, C_F = C_LANE + 1, C_LANE + 2, C_LANE + 3, C_LANE + 4
I_BIT, I_DIAG, I_N = 0, BITS, BITS + G


def build(nc, xT, x, adj, wT, cf, ci, out):
    table = nc.dram_tensor("table", (N, TW), F32).ap()
    inverse = nc.dram_tensor("inverse", (1, N), F32).ap()
    ctx = ExitStack()
    with ctx:
        def sb(name, shape, dt):
            return ctx.enter_context(nc.sbuf_tensor(name, shape, dt))

        def sem(name):
            return ctx.enter_context(nc.semaphore(name))

        whT = sb("whT", [P, KD, N], F32)
        adj_sb = sb("adj_sb", [P, 2 * NQ - 1, QC], I32)
        mask = sb("mask", [P, NQ, QC], BF16)
        bias = sb("bias", [P, 2, N], BF16)
        gat = sb("gat", [P, PAIRS, 2, TW], F32)
        gT = sb("gT", [P, 2, KD, 2, P], F32)
        prob = sb("prob", [P, 2, 2, P], F32)
        own = sb("own", [P, G], I32)
        keys = sb("keys", [P, G, NT], F32)
        base = sb("base", [P, NT], F32)
        used = sb("used", [P, NT], F32)
        small = sb("small", [P, 3], F32)
        most = sb("most", [1, 3], I32)
        topb = sb("topb", [P, RND], F32)
        topk = sb("topk", [P, G, RND], F32)
        topi = sb("topi", [P, G, RND], I32)
        bits = sb("bits", [P, 2 * RND, G, BITS], U16)
        rows = sb("rows", [P, 2, NT], U32)
        rows_now = sb("rows_now", [P, PAIRS, 2], U32)
        xyz = sb("xyz", [P, 4, D], F32)
        stats = sb("stats", [P, 6], F32)
        mv = sb("mv", [P, 2, 2], F32)
        rstd = sb("rstd", [P, 2, 2], F32)
        cf_sb = sb("cf_sb", [P, C_F], F32)
        ci_sb = sb("ci_sb", [P, I_N], I32)
        idb = sb("idb", [P, P], BF16)
        idr = sb("idr", [P, P], F32R)
        packw = sb("packw", [P, G], BF16)
        zeros = sb("zeros", [P, P], BF16)

        wT_sb = keys[:, :, :].rearrange("p g b -> p (g b)")[:, 0:KD * D].rearrange("p (k o) -> p k o", k=KD)
        den, count = small[:, 0:2], small[:, 2:3]
        ident = idr[:, :].bitcast(F32)
        x_ring = xyz[:, :, :].rearrange("p r (k n) -> p r k n", k=KD)
        unit = prob[:, :, :, :].rearrange("p a b c -> p a (b c)")
        tab = bias[:, 1, :].bitcast(F32)[:, 0:RING * TW].rearrange("p (r w) -> p r w", r=RING)
        r_row = cf_sb[:, C_ID:C_ID + P]
        factor = bits[:, 0:2, :, :].rearrange("p s g k -> p (s g k)").bitcast(F32)
        junk = gT[:, 0, 0, :, :].rearrange("p b c -> p (b c)")
        ssq, ssg = gT[:, 1, 0, 0, 0:P0], gT[:, 1, 0, 0, P0:2 * P0]

        def bank(name):
            return ctx.enter_context(nc.psum_tensor(name, [P, 512], F32))

        words_ps = [bank("words0"), bank("words1")]
        gT_ps = [bank("gT0"), bank("gT1")]
        s_ps = [bank("s0"), bank("s1")]
        o_ps = [bank("o0"), bank("o1")]

        consts_in = sem("consts_in")
        consts_ready = sem("consts_ready")
        x_in = [sem(f"x_in{k}") for k in range(XR // 2)]
        wh_done = sem("wh_done")
        tab_copied = sem("tab_copied")
        ss_ready = sem("ss_ready")
        r_ready = sem("r_ready")
        unit_ready = sem("unit_ready")
        unitT_done = sem("unitT_done")
        unitT_saved = sem("unitT_saved")
        tab_stored = [sem(f"tab_stored{k}") for k in range(RING // 2)]
        table_ready = sem("table_ready")
        adj_in = [[sem(f"adj_in{a}{q}") for q in range(NQ)] for a in range(2)]
        conv_done = sem("conv_done")
        packed = sem("packed")
        count_ready = sem("count_ready")
        words_read = sem("words_read")
        countT_done = sem("countT_done")
        most_ready = sem("most_ready")
        round_ready = sem("round_ready")
        g_ready = [sem(f"g_ready{k}") for k in range(PAIRS)]
        g_free = [sem(f"g_free{k}") for k in range(PAIRS)]
        gT_done = sem("gT_done")
        gT_saved = sem("gT_saved")
        s_done = sem("s_done")
        prob_ready = sem("prob_ready")
        tile_done = sem("tile_done")
        r_kept = sem("r_kept")
        far_ready = sem("far_ready")
        inverse_in = sem("inverse_in")
        farT_done = sem("farT_done")
        mode_ready = sem("mode_ready")
        row_in = sem("row_in")
        row_used = sem("row_used")
        corrected = sem("corrected")
        res_in = [sem("res_in0"), sem("res_in1")]
        y_read = sem("y_read")
        var_ready = sem("var_ready")
        rstd_ready = sem("rstd_ready")
        z_ready = sem("z_ready")
        stored = [sem("stored0"), sem("stored1")]
        dve_step = sem("dve_step")
        pool_step = sem("pool_step")

        def pairs_of(eng, a, tile_no):
            counted = eng.snap(tile_no)
            eng.wait_ge(consts_in, 48)
            eng.wait_ge(most_ready, counted)
            top = eng.value_load(most[0:1, a:a + 1], min_val=1, max_val=NT)
            eng.reg_add(tile_no, tile_no, 1)
            return eng.snap((top + 1) >> 1)

        def wait(eng, s, value):
            if not isinstance(value, int) or value > 0:
                eng.wait_ge(s, value)

        def tiles(eng, body):
            for t in range(3):
                body(t, t % 2)
            with eng.Fori(0, (NT - 6) // 2) as i:
                body(2 * i + 3, 1)
                body(2 * i + 4, 0)
            for t in range(NT - 3, NT):
                body(t, t % 2)

        def buffer(a, b):
            return PAIRS - 1 - b if a else b

        def pass_of(r):
            return nc.s_assert_within(r, 0, NT // (2 * PAIRS) - 1, skip_runtime_bounds_check_because="a lane has 64 columns")

        def ring(t):
            return xyz[:, t % 4, :] if isinstance(t, int) else xyz[:, bass.ds(t & 3, 1), :].rearrange("p r d -> p (r d)")

        def adj_part(a, q):
            return adj_sb[:, 2 * NQ - 2 if q == NQ - 1 else a * (NQ - 1) + q, :]

        def half(t):
            return t // 2 if isinstance(t, int) else (t >> 1)

        block = ctx.enter_context(nc.Block())

        @block.sync
        def _(sp):
            sp.dma_start(cf_sb[:, :], cf).then_inc(consts_in, 16)
            sp.dma_start(ci_sb[:, :], ci).then_inc(consts_in, 16)
            sp.dma_start(wT_sb[:, :, :], wT.rearrange("(k p) o -> p k o", p=P)).then_inc(consts_in, 16)

            def load_adj(t, a, q):
                used = NQ * t + q + 1 - (NQ if q == NQ - 1 else 2 * NQ)
                before = 16 * (half(t) + (1 if q >= 2 else a))
                if not isinstance(t, int):
                    used, before = sp.snap(used), sp.snap(before)
                    sp.wait_ge(consts_in, 48)
                wait(sp, conv_done, used)
                if not isinstance(t, int) or t >= 2:
                    sp.wait_ge(adj_in[a if q >= 2 else 1 - a][(q - 2) % NQ], before)
                sp.dma_start(adj_part(a, q), adj[bass.ds(t * P, P), q * QC:(q + 1) * QC]).then_inc(adj_in[a][q], 16)

            def project(i, load):
                for k in range(0, P0, 2):
                    m = P0 * i + k
                    wait(sp, wh_done, m - 2)
                    sp.dma_start(x_ring[:, k % XR:k % XR + 2, :, :].rearrange("p a k n -> p a (k n)"),
                                 xT[m:m + 2, :, :, :].rearrange("a p k n -> p a (k n)")).then_inc(x_in[k % XR // 2], 16)
                    if m >= 4:
                        store(m - 4)
                    if k % 4 == 2 and m < NT - 2:
                        load(k // 4)

            def store(m):
                sp.wait_ge(r_ready, m + 2)
                k = m % RING
                sp.dma_start(table[m * P:(m + 2) * P, :].rearrange("(a p) w -> p a w", p=P), tab[:, k:k + 2, :]).then_inc(tab_stored[k // 2], 16)

            for i in range(P0):
                project(i, lambda h: load_adj(i // 4, i // 4, i % 4 * 2 + h))
            for m in (NT - 4, NT - 2):
                store(m)
            for k in range(RING // 2):
                sp.wait_ge(tab_stored[k], 16 * NT // RING)
            sp.sem_inc(table_ready, 1)

            place = sp.alloc_register("place")

            def load_res(t, a):
                gone = 16 * half(t - 2)
                if isinstance(t, int):
                    to = ring(t)
                else:
                    sp.reg_mov(place, t & 3)
                    at = nc.s_assert_within(sp.snap(place), 0, 3, skip_runtime_bounds_check_because="two bits")
                    to = xyz[:, bass.ds(at, 1), :].rearrange("p r d -> p (r d)")
                wait(sp, y_read, t - 1)
                if not isinstance(t, int) or t >= 4:
                    sp.wait_ge(stored[a], gone)
                sp.dma_start(to, x[bass.ds(t * P, P), :]).then_inc(res_in[a], 16)

            def store_out(t, a):
                sp.wait_ge(z_ready, t + 1)
                sp.dma_start(out[bass.ds(t * P, P), :], ring(t)).then_inc(stored[a], 16)

            load_adj(1, 1, NQ - 1)
            for t in range(2, 8):
                for q in range(NQ):
                    load_adj(t, t % 2, q)
                if t >= 4:
                    load_res(t - 4, t % 2)
            with sp.Fori(4, NT // 2) as i:
                for a in range(2):
                    store_out(2 * i + a - 8, a)
                    for q in range(NQ):
                        load_adj(2 * i + a, a, q)
                    load_res(2 * i + a - 4, a)
            for t in range(NT, NT + 8):
                store_out(t - 8, t % 2)
                if t < NT + 4:
                    load_res(t - 4, t % 2)
            for a in range(2):
                sp.wait_ge(stored[a], 16 * NT // 2)

        @block.gpsimd
        def _(pool):
            pool.memset(gat[:, :, :, :], 0.0).then_inc(consts_ready, 1)
            pool.memset(tab[:, :, ONE:ONE + 1], 1.0).then_inc(pool_step, 1)
            pool.memset(zeros[:, :], 0.0).then_inc(consts_ready, 1)

            def project(i):
                for k in range(P0):
                    m = P0 * i + k
                    pool.sem_clear(pool_step)
                    pool.wait_ge(ss_ready, m + 1)
                    pool.tensor_tensor(ssg[:, k:k + 1], ssq[:, k:k + 1], cf_sb[:, C_TINY:C_TINY + 1], ALU.add).then_inc(pool_step, 1)
                    pool.wait_ge(pool_step, 1)
                    pool.tensor_tensor(tab[:, k % RING, RN:RN + 1], ssg[:, k:k + 1], cf_sb[:, C_HALF:C_HALF + 1], ALU.pow).then_inc(r_ready, 1)

            pool.wait_ge(pool_step, 1)
            pool.wait_ge(consts_in, 48)
            project(0)
            with pool.Fori(1, P0) as i:
                project(i)

            pool.wait_ge(table_ready, 1)
            tile_no = pool.alloc_register("tile_no")
            pool.reg_mov(tile_no, 1)
            rounds = pool.alloc_register("rounds")
            pool.reg_mov(rounds, 1)
            uses = [pool.alloc_register(f"uses{k}") for k in range(PAIRS)]
            for u in uses:
                pool.reg_mov(u, 1)

            def gather(a, r, b):
                k = buffer(a, b)
                pool.sem_clear(pool_step)
                if b % (RND // 2) == 0:
                    pool.wait_ge(round_ready, pool.snap(rounds))
                    pool.reg_add(rounds, rounds, 1)
                pool.wait_ge(g_free[k], pool.snap(uses[k]))
                pool.tensor_copy(rows_now[:, k, :], rows[:, a, bass.ds((r * PAIRS + b) * 2, 2)]).then_inc(pool_step, 1)
                pool.wait_ge(pool_step, 1)
                for s in range(2):
                    pool.indirect_dma_start(
                        out=gat[:, k, s, :], out_offset=None, in_=table,
                        in_offset=bass.IndirectOffsetOnAxis(ap=rows_now[:, k, s:s + 1], axis=0),
                        bounds_check=N - 1, oob_is_err=False).then_inc(g_ready[k], 16)
                pool.reg_add(uses[k], uses[k], 1)

            def inverse_dev(t, a):
                pool.sem_clear(pool_step)
                pool.wait_ge(var_ready, t + 1)
                pool.tensor_tensor(rstd[:, a, 0:1], mv[:, a, 1:2], cf_sb[:, C_EPS:C_EPS + 1], ALU.add).then_inc(pool_step, 1)
                pool.wait_ge(pool_step, 1)
                pool.tensor_tensor(rstd[:, a, 1:2], rstd[:, a, 0:1], cf_sb[:, C_HALF:C_HALF + 1], ALU.pow).then_inc(rstd_ready, 1)

            pool.wait_ge(mode_ready, 1)
            slow = pool.value_load(most[0:1, 2:3], min_val=0, max_val=1)

            with pool.If(slow > 0):
                pool.dma_start(inverse[0:1, :].rearrange("o (n w) -> (o n) w", w=1), table[:, RN:RN + 1], allow_slow_non_contiguous=True).then_inc(inverse_in, 16)
                pool.wait_ge(inverse_in, 16)

            def load_row(t):
                wait(pool, row_used, t)
                pool.dma_start(r_row, inverse[0:1, bass.ds(t * P, P)].broadcast_to([P, P])).then_inc(row_in, 16)

            def tile(t, a):
                if not isinstance(t, int) or t >= 3:
                    inverse_dev(t - 3, 1 - a)
                pairs = pairs_of(pool, a, tile_no)
                with pool.If(slow > 0):
                    load_row(t)

                def step(r, b):
                    with pool.If(r * PAIRS + b < pairs):
                        gather(a, r, b)
                        if b + 1 < PAIRS:
                            step(r, b + 1)

                with pool.Fori(0, (pairs + (PAIRS - 1)) >> 3) as r:
                    r = pass_of(r)
                    gather(a, r, 0)
                    step(r, 1)

            tiles(pool, tile)
            for t in range(NT - 3, NT):
                inverse_dev(t, t % 2)

        @block.vector
        def _(dve):
            step = [0]

            def restart():
                dve.sem_clear(dve_step)
                step[0] = 0

            def nothing(q):
                pass

            def then(ins, convert=nothing, q=None):
                step[0] += 1
                ins.then_inc(dve_step, 1)
                convert(q)
                dve.wait_ge(dve_step, step[0])

            dve.wait_ge(consts_in, 48)
            dve.tensor_copy(idb[:, :], cf_sb[:, C_ID:C_ID + P]).then_inc(consts_ready, 1)
            dve.tensor_copy(idr[:, :], cf_sb[:, C_ID:C_ID + P]).then_inc(consts_ready, 1)
            dve.tensor_copy(packw[:, :], cf_sb[:, C_PACK:C_PACK + G]).then_inc(consts_ready, 1)

            def normalise(m, k):
                dve.wait_ge(r_ready, m + 1)
                wait(dve, unitT_done, m - 1)
                dve.tensor_scalar(unit[:, k % 2, :], tab[:, k, 0:D], tab[:, k, RN:RN + 1], None, ALU.mult).then_inc(unit_ready, 1)
                dve.tensor_copy(base[:, bass.ds(m, 1)], tab[:, k, RN:RN + 1]).then_inc(r_kept, 1)

            def convert_part(t, a, q):
                dve.wait_ge(adj_in[a][q], 16 * (half(t) + 1))
                wait(dve, packed, NQ * t + q + 1 - NQ)
                dve.tensor_scalar(mask[:, q, :], adj_part(a, q), 0, None, ALU.is_gt).then_inc(conv_done, 1)

            def project(i, convert=nothing):
                for k in range(P0):
                    m = P0 * i + k
                    dve.wait_ge(wh_done, m + 1)
                    wait(dve, tab_stored[k // 2], 16 * i)
                    dve.tensor_copy(tab[:, k, 0:D], s_ps[k % 2][:, 0:D]).then_inc(tab_copied, 1)
                    if not isinstance(m, int) or m >= 2:
                        normalise(m - 2, (k - 2) % P0)
                    convert(k)

            def convert_first(q):
                convert_part(0, 0, q)

            def convert_second(q):
                if q < NQ - 1:
                    convert_part(1, 1, q)

            project(0)
            with dve.Fori(1, P0 // 2) as i:
                project(i)
            project(P0 // 2, convert_first)
            with dve.Fori(P0 // 2 + 1, P0 - 1) as i:
                project(i)
            project(P0 - 1, convert_second)
            for m in range(NT - 2, NT):
                normalise(m, m % P0)

            def select_round(a, r, convert=nothing):
                dve.max(topb[:, :], base[:, :])
                for g in range(G):
                    last = dve.max(topk[:, g, :], keys[:, g, :])
                then(last, convert, 0)
                dve.tensor_scalar(rows[:, a, bass.ds(r * RND, RND)], topb[:, :], -1.0 / 512, cf_sb[:, C_LANE:C_LANE + 1], ALU.mult, ALU.add)
                then(dve.tensor_copy(topi[:, :, :], topk[:, :, :]))
                then(dve.tensor_tensor(bits[:, 0:RND, :, :],
                                       topi[:, :, :].bitcast(U16)[:, :, 0:2 * RND:2].rearrange("p g (s o) -> p s g o", o=1).broadcast_to([P, RND, G, BITS]),
                                       ci_sb[:, I_BIT:I_BIT + BITS].bitcast(U16)[:, 0:2 * BITS:2].rearrange("p (u v k) -> p u v k", u=1, v=1).broadcast_to([P, RND, G, BITS]),
                                       ALU.bitwise_and), convert, 1)
                dve.tensor_scalar(bias[:, a, bass.ds(r * RND * P, RND * P)], bits[:, 0:RND, :, :].rearrange("p s g k -> p (s g k)"),
                                  0.0, MASKED, ALU.is_equal, ALU.mult).then_inc(round_ready, 1)
                convert(2)

            def next_round(a, r):
                then(dve.scalar_tensor_tensor(keys[:, :, :], base[:, :].rearrange("p (o b) -> p o b", o=1).broadcast_to([P, G, NT]),
                                              topb[:, RND - 1:RND], keys[:, :, :], ALU.is_lt, ALU.mult))
                then(dve.scalar_tensor_tensor(base[:, :], base[:, :], topb[:, RND - 1:RND], base[:, :], ALU.is_lt, ALU.mult))
                select_round(a, r)

            def make_keys(t, a, convert=nothing):
                restart()
                dve.wait_ge(packed, NQ * t + NQ)
                by_block = words_ps[a][:, :].rearrange("p (b g) -> p b g", g=G)
                dve.tensor_copy(own[:, :], words_ps[a][:, bass.ds(t * G, G)])
                then(dve.tensor_reduce(used[:, :], by_block, AX.X, ALU.max), convert, 4)
                here = used[:, bass.ds(t, 1)]
                dve.tensor_tensor(own[:, :], own[:, :], ci_sb[:, I_DIAG:I_DIAG + G], ALU.bitwise_or)
                then(dve.tensor_scalar(here, here, 1.0, None, ALU.add))
                then(dve.tensor_scalar(base[:, :], used[:, :], 0.0, None, ALU.is_gt), convert, 5)
                dve.tensor_reduce(count[:, :], base[:, :], AX.X, ALU.add).then_inc(count_ready, 1)
                then(dve.tensor_tensor(base[:, :], base[:, :], cf_sb[:, C_BLK:C_BLK + NT], ALU.mult), convert, 6)
                then(dve.tensor_tensor(keys[:, :, :], words_ps[a][:, :].rearrange("p (b g) -> p g b", g=G),
                                       base[:, :].rearrange("p (o b) -> p o b", o=1).broadcast_to([P, G, NT]), ALU.add))
                dve.sem_inc(words_read, 1)
                then(dve.tensor_scalar(keys[:, :, bass.ds(t, 1)].rearrange("p g o -> p (g o)"), own[:, :], base[:, bass.ds(t, 1)], None, ALU.add), convert, 7)

            def select(t, a, convert=nothing):
                restart()
                if isinstance(t, int) and t == 1:
                    dve.wait_ge(table_ready, 1)
                wait(dve, tile_done, t - 1)
                dve.wait_ge(countT_done, t + 1)
                dve.tensor_reduce(most[0:1, a:a + 1], words_ps[a][0:1, 0:P], AX.X, ALU.max).then_inc(most_ready, 1)
                select_round(a, 0, convert)
                top = dve.value_load(most[0:1, a:a + 1], min_val=1, max_val=NT)
                with dve.If(top > RND):
                    next_round(a, 1)
                    with dve.If(top > 2 * RND):
                        with dve.Fori(2, (top + (RND - 1)) >> 3) as r:
                            r = nc.s_assert_within(r, 2, NT // RND - 1, skip_runtime_bounds_check_because="a lane has 64 columns")
                            restart()
                            next_round(a, r)
                convert(3)

            def residual(t, a):
                restart()
                dve.wait_ge(tile_done, t + 1)
                dve.wait_ge(res_in[a], 16 * (half(t) + 1))
                then(dve.reciprocal(den[:, a:a + 1], o_ps[a][:, ONE:ONE + 1]))
                then(dve.scalar_tensor_tensor(ring(t), o_ps[a][:, 0:D], den[:, a:a + 1], ring(t), ALU.mult, ALU.add))
                dve.sem_inc(y_read, 1)
                then(dve.bn_stats(stats[:, :], ring(t)))
                dve.bn_aggr(mv[:, a, :], stats[:, :]).then_inc(var_ready, 1)

            def scale_rows(t, a):
                dve.wait_ge(rstd_ready, t + 1)
                wait(dve, stored[a], 16 * half(t))
                dve.tensor_scalar(ring(t), ring(t), mv[:, a, 0:1], rstd[:, a, 1:2], ALU.subtract, ALU.mult).then_inc(z_ready, 1)

            seen = dve.alloc_register("seen")
            dve.reg_mov(seen, 2)
            row_loads = dve.alloc_register("row_loads")
            dve.reg_mov(row_loads, 16)

            def correct(t, a):
                with dve.If(slow > 0):
                    restart()
                    loaded = dve.snap(row_loads)
                    dve.wait_ge(consts_in, 48)
                    dve.wait_ge(row_in, loaded)
                    top = dve.value_load(most[0:1, a:a + 1], min_val=1, max_val=NT)
                    pairs = dve.snap((top + 1) >> 1)
                    then(dve.tensor_copy(topb[:, 0:1], topb[:, 1:2]))
                    dve.reg_add(row_loads, row_loads, 16)

                    def one(j, b):
                        k = PAIRS - 1 - (j & (PAIRS - 1)) if a else j & (PAIRS - 1)
                        restart()
                        dve.wait_ge(s_done, dve.snap(seen))
                        for s in range(2):
                            r_j = gat[:, bass.ds(k, 1), s, RN:RN + 1].rearrange("p o w -> p (o w)")
                            ps = s_ps[b][:, s * P:(s + 1) * P]
                            then(dve.tensor_scalar(factor, r_row, r_j, None, ALU.mult))
                            then(dve.tensor_scalar(factor, factor, EPS_SIM, 1.0, ALU.mult, ALU.add))
                            then(dve.reciprocal(factor, factor))
                            then(dve.tensor_tensor(factor, ps, factor, ALU.mult))
                            then(dve.tensor_scalar(ps, factor, FLOOR, None, ALU.max))
                        dve.sem_inc(corrected, 1)
                        dve.reg_add(seen, seen, 1)

                    with dve.Fori(0, (pairs + 1) >> 1) as r:
                        r = nc.s_assert_within(r, 0, NT // 4 - 1, skip_runtime_bounds_check_because="a lane has 64 columns")
                        one(2 * r, 0)
                        with dve.If(2 * r + 1 < pairs):
                            one(2 * r + 1, 1)
                    dve.sem_inc(row_used, 1)

            def tile(t, a):
                last = isinstance(t, int) and t + 2 >= NT

                def convert(q):
                    if not last:
                        convert_part(t + 2, a, q)

                if not isinstance(t, int) or t >= 4:
                    scale_rows(t - 4, a)
                select(t, a, convert)
                if not isinstance(t, int) or t >= 1:
                    correct(t - 1, 1 - a)
                if not isinstance(t, int) or t >= 2:
                    residual(t - 2, a)
                if not isinstance(t, int) or t + 1 < NT:
                    make_keys(t + 1, 1 - a, convert)

            restart()
            dve.wait_ge(r_kept, NT)
            then(dve.tensor_reduce(count[:, :], base[:, :], AX.X, ALU.max))
            dve.sem_inc(far_ready, 1)
            convert_part(1, 1, NQ - 1)
            dve.wait_ge(farT_done, 1)
            then(dve.tensor_reduce(den[0:1, 0:1], o_ps[0][0:1, 0:P], AX.X, ALU.max))
            then(dve.tensor_scalar(most[0:1, 2:3], den[0:1, 0:1], FAR, None, ALU.is_gt))
            slow = dve.value_load(most[0:1, 2:3], min_val=0, max_val=1)
            dve.sem_inc(mode_ready, 1)
            dve.sem_inc(corrected, 1)
            with dve.If(slow == 0):
                dve.sem_inc(corrected, PLENTY)
            make_keys(0, 0)
            for t in range(4):
                tile(t, t % 2)
            with dve.Fori(2, NT // 2 - 1) as i:
                tile(2 * i, 0)
                tile(2 * i + 1, 1)
            for t in range(NT - 2, NT):
                tile(t, t % 2)
            correct(NT - 1, (NT - 1) % 2)
            for t in range(NT, NT + 4):
                scale_rows(t - 4, t % 2)
                if t < NT + 2:
                    residual(t - 2, t % 2)

        @block.scalar
        def _(act):
            def save_unitT(m, k):
                act.wait_ge(unitT_done, m + 1)
                act.activation(whT[:, :, bass.ds(m * P, P)], gT_ps[k % 2][:, 0:D].rearrange("p (k n) -> p k n", k=KD), ACT.Copy).then_inc(unitT_saved, 1)

            def project(i):
                for k in range(P0):
                    m = P0 * i + k
                    act.wait_ge(tab_copied, m + 1)
                    wait(act, ss_ready, m)
                    wait(act, r_ready, m - P0 + 1)
                    act.activation(junk, tab[:, k, 0:D], ACT.Square, accum_out=ssq[:, k:k + 1]).then_inc(ss_ready, 1)
                    if not isinstance(m, int) or m >= 3:
                        save_unitT(m - 3, (k - 3) % P0)

            project(0)
            with act.Fori(1, P0) as i:
                project(i)
            for m in range(NT - 3, NT):
                save_unitT(m, m % P0)
            act.wait_ge(r_ready, NT)

            pair = act.alloc_register("pair")
            act.reg_mov(pair, 1)
            tile_no = act.alloc_register("tile_no")
            act.reg_mov(tile_no, 1)
            act.activation(junk[0:1, 0:1], junk[0:1, 0:1], ACT.Copy).then_inc(prob_ready, 1)
            act.wait_ge(prob_ready, 1)

            def save_gT(b):
                act.wait_ge(gT_done, act.snap(pair))
                act.activation(gT[:, b % 2, :, :, :].rearrange("p k s n -> p (k s n)"), gT_ps[b % 2][:, :], ACT.Copy).then_inc(gT_saved, 1)

            def exps(a, b):
                act.wait_ge(s_done, act.snap(pair))
                act.wait_ge(corrected, act.snap(pair))
                for s in range(2):
                    last = act.activation(prob[:, b % 2, s, :], s_ps[b % 2][:, s * P:(s + 1) * P], ACT.Exp, scale=gat[:, buffer(a, b), s, RN:RN + 1])
                last.then_inc(prob_ready, 1)

            def tile(t, a):
                pairs = pairs_of(act, a, tile_no)

                def step(r, b):
                    with act.If(r * PAIRS + b < pairs):
                        save_gT(b)
                        exps(a, b - 1)
                        act.reg_add(pair, pair, 1)
                        if b + 1 < PAIRS:
                            step(r, b + 1)
                        else:
                            with act.If(r * PAIRS + PAIRS == pairs):
                                exps(a, b)
                    with act.Else():
                        exps(a, b - 1)

                with act.Fori(0, (pairs + (PAIRS - 1)) >> 3) as r:
                    with act.If(r > 0):
                        save_gT(0)
                        exps(a, PAIRS - 1)
                    with act.Else():
                        save_gT(0)
                    act.reg_add(pair, pair, 1)
                    step(r, 1)

            for t in range(2):
                tile(t, t % 2)
            with act.Fori(1, NT // 2) as i:
                tile(2 * i, 0)
                tile(2 * i + 1, 1)

        @block.tensor
        def _(pe):
            pe.wait_ge(consts_in, 48)
            pe.wait_ge(consts_ready, 5)

            def unitT(m, k):
                pe.wait_ge(unit_ready, m + 1)
                wait(pe, unitT_saved, m - 1)
                for h in range(KD):
                    last = pe.transpose(gT_ps[k % 2][:, h * P:(h + 1) * P], unit[:, k % 2, h * P:(h + 1) * P], ident)
                last.then_inc(unitT_done, 1)

            def project(i):
                for k in range(P0):
                    m = P0 * i + k
                    pe.wait_ge(x_in[k % XR // 2], 16 * (2 * i + k // XR + 1))
                    wait(pe, tab_copied, m - 1)
                    for h in range(KD):
                        last = pe.matmul(s_ps[k % 2][:, 0:D], x_ring[:, k % XR, h, :], wT_sb[:, h, :], start=(h == 0), stop=(h == KD - 1))
                    last.then_inc(wh_done, 1)
                    if not isinstance(m, int) or m >= 3:
                        unitT(m - 3, (k - 3) % P0)

            def pack(t, a):
                for q in range(NQ):
                    pe.wait_ge(conv_done, NQ * t + q + 1)
                    for b in range(QB):
                        at = (q * QB + b) * G
                        last = pe.matmul(words_ps[a][:, at:at + G], mask[:, q, b * P:(b + 1) * P], packw[:, :], start=True, stop=True)
                    last.then_inc(packed, 1)

            project(0)
            with pe.Fori(1, P0 // 2 + 1) as i:
                project(i)
            pack(0, 0)
            with pe.Fori(P0 // 2 + 1, P0) as i:
                project(i)
            for m in range(NT - 3, NT):
                unitT(m, m % P0)
            pe.wait_ge(unitT_saved, NT)

            for k in range(PAIRS):
                pe.matmul(o_ps[0][:, k:k + 1], zeros[:, :], zeros[:, 0:1], start=True, stop=True).then_inc(g_free[k], 1)
            pe.matmul(o_ps[0][:, PAIRS:PAIRS + 1], zeros[:, :], zeros[:, 0:1], start=True, stop=True).then_inc(s_done, 1)

            pe.wait_ge(far_ready, 1)
            pe.matmul(o_ps[0][0:1, 0:P], count[:, :], ident, start=True, stop=True).then_inc(farT_done, 1)

            pair = pe.alloc_register("pair")
            landed = [pe.alloc_register(f"landed{k}") for k in range(PAIRS)]
            pe.reg_mov(pair, 0)
            tile_no = pe.alloc_register("tile_no")
            pe.reg_mov(tile_no, 1)
            for u in landed:
                pe.reg_mov(u, 32)

            def transposes(a, b):
                k = buffer(a, b)
                pe.wait_ge(g_ready[k], pe.snap(landed[k]))
                for s in range(2):
                    for h in range(KD):
                        last = pe.transpose(gT_ps[b % 2][:, (2 * h + s) * P:(2 * h + s + 1) * P].bitcast(F32R),
                                            gat[:, k, s, h * P:(h + 1) * P].bitcast(F32R), idr[:, :])
                last.then_inc(gT_done, 1)
                pe.reg_add(landed[k], landed[k], 32)

            def products(t, a, r, b, n):
                pe.wait_ge(gT_saved, n)
                ps = s_ps[b % 2]
                pe.matmul(ps[:, 0:2 * P], idb[:, :], bias[:, a, bass.ds((r * PAIRS + b) * 2 * P, 2 * P)], start=True, stop=False, skip_group_check=True)
                for s in range(2):
                    for h in range(KD):
                        last = pe.matmul(ps[:, s * P:(s + 1) * P], gT[:, b % 2, h, s, :], whT[:, h, bass.ds(t * P, P)],
                                         start=False, stop=(h == KD - 1), skip_group_check=True)
                last.then_inc(s_done, 1)

            def add_up(a, b, n):
                pe.wait_ge(prob_ready, n)
                for s in range(2):
                    last = pe.matmul(o_ps[a][:, 0:D + 1], prob[:, b % 2, s, :], gat[:, buffer(a, b), s, 0:D + 1], start=False, stop=False, skip_group_check=True)
                last.then_inc(g_free[buffer(a, b)], 1)

            def attend(t, a, pairs):
                def pack_ahead():
                    if not isinstance(t, int) or t + 2 < NT:
                        pack(t + 2, a)

                def finish(r, b):
                    more = not isinstance(t, int) or t + 1 < NT
                    held = buffer(1 - a, 0) == buffer(a, b)
                    if b >= 1:
                        products(t, a, r, b, pe.snap(pair))
                        add_up(a, b - 1, pe.snap(pair))
                    else:
                        with pe.If(pairs > 1):
                            products(t, a, r, b, pe.snap(pair))
                            add_up(a, PAIRS - 1, pe.snap(pair))
                        with pe.Else():
                            pack_ahead()
                    if more and not held:
                        transposes(1 - a, 0)
                    add_up(a, b, pe.snap(pair) + 1)
                    pe.matmul(o_ps[a][:, D:D + 2], zeros[:, :], zeros[:, 0:2], start=False, stop=True, skip_group_check=True).then_inc(tile_done, 1)
                    if more and held:
                        transposes(1 - a, 0)
                    pe.reg_add(pair, pair, 1)

                def step(r, b):
                    with pe.If(r * PAIRS + b < pairs):
                        if b >= 2:
                            products(t, a, r, b - 1, pe.snap(pair))
                            transposes(a, b)
                            add_up(a, b - 2, pe.snap(pair))
                        else:
                            with pe.If(r > 0):
                                products(t, a, r, b - 1, pe.snap(pair))
                                transposes(a, b)
                                add_up(a, PAIRS - 1, pe.snap(pair))
                            with pe.Else():
                                transposes(a, b)
                                pack_ahead()
                        pe.reg_add(pair, pair, 1)
                        if b + 1 < PAIRS:
                            step(r, b + 1)
                        else:
                            with pe.If(r * PAIRS + PAIRS == pairs):
                                finish(r, b)
                    with pe.Else():
                        finish(r, b - 1)

                with pe.Fori(0, (pairs + (PAIRS - 1)) >> 3) as r:
                    r = pass_of(r)
                    with pe.If(r > 0):
                        products(t, a, pass_of(r - 1), PAIRS - 1, pe.snap(pair))
                        transposes(a, 0)
                        add_up(a, PAIRS - 2, pe.snap(pair))
                        pe.reg_add(pair, pair, 1)
                    step(r, 1)

            def transpose_count(t, a):
                pe.wait_ge(count_ready, t + 1)
                pe.wait_ge(words_read, t + 1)
                pe.matmul(words_ps[a][0:1, 0:P], count[:, :], ident, start=True, stop=True).then_inc(countT_done, 1)

            def tile(t, a):
                pairs = pairs_of(pe, a, tile_no)
                if not isinstance(t, int) or t + 1 < NT:
                    transpose_count(t + 1, 1 - a)
                wait(pe, y_read, t - 1)
                pe.matmul(o_ps[a][:, 0:D + 2], zeros[:, :], zeros[:, 0:1].broadcast_to([P, D + 2]), start=True, stop=False, skip_group_check=True)
                products(t, a, 0, 0, pe.snap(pair))
                attend(t, a, pairs)

            transpose_count(0, 0)
            pack(1, 1)
            transposes(0, 0)
            pe.reg_add(pair, pair, 1)
            tiles(pe, tile)


def kernel(x, adj, L0_gnn_W):
    from concourse import bacc
    from concourse.bass_utils import run_bass_kernel_spmd

    cf = np.zeros((P, C_F), np.float32)
    lane = np.arange(P)
    cf[:, C_ID:C_ID + P] = np.eye(P)
    cf[:, C_BLK:C_BLK + NT] = (NT - np.arange(NT)) * 65536.0
    cf[lane, C_PACK + lane // BITS] = 2.0 ** (lane % BITS)
    cf[:, C_LANE] = N + lane
    cf[:, C_HALF], cf[:, C_TINY], cf[:, C_EPS] = -0.5, TINY, EPS_LN
    ci = np.zeros((P, I_N), np.int32)
    ci[:, I_BIT:I_BIT + BITS] = 1 << np.arange(BITS)
    ci[lane, I_DIAG + lane // BITS] = 1 << (lane % BITS)

    x, adj, w = np.asarray(x), np.asarray(adj), np.asarray(L0_gnn_W)
    arrays = {
        "xT": np.ascontiguousarray(x.reshape(NT, P, KD, P).transpose(0, 3, 2, 1)),
        "x": np.ascontiguousarray(x),
        "adj": np.ascontiguousarray(adj),
        "wT": np.ascontiguousarray(w.T),
        "cf": cf,
        "ci": ci,
    }
    nc = bacc.Bacc("TRN2", target_bir_lowering=False, num_devices=1)
    args = [nc.dram_tensor(n, a.shape, mybir.dt.from_np(a.dtype), kind="ExternalInput").ap() for n, a in arrays.items()]
    out = nc.dram_tensor("out", (N, D), F32, kind="ExternalOutput").ap()
    build(nc, *args, out)
    return run_bass_kernel_spmd(nc, [arrays], core_ids=[0]).results[0]["out"]
```
